# Optimizing a Trainium2 kernel written in Bass

```python
import numpy as np
import jax
import jax.numpy as jnp

def _softmax(x, axis=-1):
    return jax.nn.softmax(x, axis=axis)

def _gelu(x):
    return jax.nn.gelu(x, approximate=True)

def _silu(x):
    return jax.nn.silu(x)

def _sigmoid(x):
    return jax.nn.sigmoid(x)

def _layernorm(x, axis=-1, eps=1e-05):
    m = jnp.mean(x, axis=axis, keepdims=True)
    v = jnp.var(x, axis=axis, keepdims=True)
    return (x - m) / jnp.sqrt(v + eps)

def _scatter_add(tgt, idx, src, axis=0):
    return tgt.at[idx].add(src)

def _segment_sum(src, seg, n):
    return jax.ops.segment_sum(src, seg, n)
kernel_name = 'mk_vit_tower_postln_d1_tok_img256_r4_55465c'

def setup_inputs(seed: int=0):
    np.random.seed(seed)
    _w = jnp.asarray

    def _rec_inputs():
        import jax
        import jax.numpy as jnp
        _rk = jax.random.key(seed)
        x = 7.22013e-05 + 1.00017 * jax.random.normal(jax.random.fold_in(_rk, 1), (4, 1, 1024, 64), jnp.float32)
        return x
    x = _rec_inputs()

    def _L0_tok_setup():
        import jax, jax.numpy as jnp
        import numpy as np
        T, D_IN, D_INT, D_OUT, B = (1024, 64, 64, 64, 8)
        key = jax.random.key(seed)
        ks = jax.random.split(key, 12)
        s_in = 1.0 / np.sqrt(D_IN)
        s_int = 1.0 / np.sqrt(D_INT)
        return {'x_batched': jax.random.normal(ks[0], (B, 1, T, D_IN), dtype=jnp.float32), 'd_gamma_batched': jax.random.uniform(ks[1], (T, T), dtype=jnp.float32), 'Wq': jax.random.uniform(ks[2], (D_IN, D_INT), jnp.float32, -s_in, s_in), 'bq': jax.random.uniform(ks[3], (D_INT,), jnp.float32, -s_in, s_in), 'Wk': jax.random.uniform(ks[4], (D_IN, D_INT), jnp.float32, -s_in, s_in), 'bk': jax.random.uniform(ks[5], (D_INT,), jnp.float32, -s_in, s_in), 'Wv': jax.random.uniform(ks[6], (D_IN, D_INT), jnp.float32, -s_in, s_in), 'bv': jax.random.uniform(ks[7], (D_INT,), jnp.float32, -s_in, s_in), 'Wo': jax.random.uniform(ks[8], (D_INT, D_OUT), jnp.float32, -s_int, s_int), 'bo': jax.random.uniform(ks[9], (D_OUT,), jnp.float32, -s_int, s_int), 'prelu_a': jnp.float32(0.25)}
    _L0_tok_all = _L0_tok_setup()
    _L0_tok_in = {k: v for k, v in _L0_tok_all.items() if k in ('d_gamma_batched', 'Wq', 'bq', 'Wk', 'bk', 'Wv', 'bv', 'Wo', 'bo', 'prelu_a')}
    del _L0_tok_all

    def _L0_attn_setup():
        import jax, jax.numpy as jnp
        import numpy as np
        B, T, D = (4, 1024, 64)
        EXPAND, D_STATE = (2, 16)
        INNER = D * EXPAND
        key = jax.random.key(seed)
        ks = jax.random.split(key, 8)
        s = 0.02
        return {'x': jax.random.normal(ks[0], (B, T, D), jnp.float32), 'W_in': jax.random.normal(ks[1], (D, 2 * INNER), jnp.float32) * s, 'b_in': jnp.zeros((2 * INNER,), jnp.float32), 'W_conv': jax.random.normal(ks[2], (INNER, INNER), jnp.float32) * s, 'b_conv': jnp.zeros((INNER,), jnp.float32), 'A_log': jax.random.normal(ks[3], (INNER, D_STATE), jnp.float32) * 0.01, 'W_bc': jax.random.normal(ks[4], (INNER, 2 * D_STATE), jnp.float32) * s, 'b_bc': jnp.zeros((2 * D_STATE,), jnp.float32), 'W_dt': jax.random.normal(ks[5], (INNER, INNER), jnp.float32) * s, 'b_dt': jnp.zeros((INNER,), jnp.float32), 'W_out': jax.random.normal(ks[6], (INNER, D), jnp.float32) * s, 'b_out': jnp.zeros((D,), jnp.float32)}
    _L0_attn_all = _L0_attn_setup()
    _L0_attn_in = {k: v for k, v in _L0_attn_all.items() if k in ('W_in', 'b_in', 'W_conv', 'b_conv', 'A_log', 'W_bc', 'b_bc', 'W_dt', 'b_dt', 'W_out', 'b_out')}
    del _L0_attn_all

    def _L0_ffn_setup():
        import jax, jax.numpy as jnp
        import numpy as np
        B, T, IN_DIM = (64, 64, 64)
        HID, OUT_DIM = (128, 64)
        N_LAYERS, N_EXPERTS, N_SHARED = (2, 16, 1)
        key = jax.random.key(seed)
        ks = jax.random.split(key, 10)
        s = 0.02
        x = jax.random.normal(ks[0], (B, T, IN_DIM), dtype=jnp.float32)
        route_id = jax.random.randint(ks[1], (B,), 0, N_EXPERTS)
        Wi = jax.random.normal(ks[2], (HID, IN_DIM), dtype=jnp.float32) * s
        bi = jnp.zeros((HID,), dtype=jnp.float32)
        Wr = jax.random.normal(ks[3], (N_LAYERS, N_EXPERTS, HID, HID), dtype=jnp.float32) * s
        br = jax.random.normal(ks[4], (N_LAYERS, N_EXPERTS, HID), dtype=jnp.float32) * s
        Ws = jax.random.normal(ks[5], (N_LAYERS, N_SHARED, HID, HID), dtype=jnp.float32) * s
        bs = jax.random.normal(ks[6], (N_LAYERS, N_SHARED, HID), dtype=jnp.float32) * s
        Wo = jax.random.normal(ks[7], (OUT_DIM, HID), dtype=jnp.float32) * s
        bo = jnp.zeros((OUT_DIM,), dtype=jnp.float32)
        return {'x': x, 'route_id': route_id, 'Wi': Wi, 'bi': bi, 'Wr': Wr, 'br': br, 'Ws': Ws, 'bs': bs, 'Wo': Wo, 'bo': bo}
    _L0_ffn_all = _L0_ffn_setup()
    _L0_ffn_in = {k: v for k, v in _L0_ffn_all.items() if k in ('route_id', 'Wi', 'bi', 'Wr', 'br', 'Ws', 'bs', 'Wo', 'bo')}
    del _L0_ffn_all
    return {'x': x, 'L0_tok_d_gamma_batched': _L0_tok_in['d_gamma_batched'], 'L0_tok_Wq': _L0_tok_in['Wq'], 'L0_tok_bq': _L0_tok_in['bq'], 'L0_tok_Wk': _L0_tok_in['Wk'], 'L0_tok_bk': _L0_tok_in['bk'], 'L0_tok_Wv': _L0_tok_in['Wv'], 'L0_tok_bv': _L0_tok_in['bv'], 'L0_tok_Wo': _L0_tok_in['Wo'], 'L0_tok_bo': _L0_tok_in['bo'], 'L0_tok_prelu_a': _L0_tok_in['prelu_a'], 'L0_attn_W_in': _L0_attn_in['W_in'], 'L0_attn_b_in': _L0_attn_in['b_in'], 'L0_attn_W_conv': _L0_attn_in['W_conv'], 'L0_attn_b_conv': _L0_attn_in['b_conv'], 'L0_attn_A_log': _L0_attn_in['A_log'], 'L0_attn_W_bc': _L0_attn_in['W_bc'], 'L0_attn_b_bc': _L0_attn_in['b_bc'], 'L0_attn_W_dt': _L0_attn_in['W_dt'], 'L0_attn_b_dt': _L0_attn_in['b_dt'], 'L0_attn_W_out': _L0_attn_in['W_out'], 'L0_attn_b_out': _L0_attn_in['b_out'], 'L0_ffn_route_id': _L0_ffn_in['route_id'], 'L0_ffn_Wi': _L0_ffn_in['Wi'], 'L0_ffn_bi': _L0_ffn_in['bi'], 'L0_ffn_Wr': _L0_ffn_in['Wr'], 'L0_ffn_br': _L0_ffn_in['br'], 'L0_ffn_Ws': _L0_ffn_in['Ws'], 'L0_ffn_bs': _L0_ffn_in['bs'], 'L0_ffn_Wo': _L0_ffn_in['Wo'], 'L0_ffn_bo': _L0_ffn_in['bo']}

def reference(x, L0_tok_d_gamma_batched, L0_tok_Wq, L0_tok_bq, L0_tok_Wk, L0_tok_bk, L0_tok_Wv, L0_tok_bv, L0_tok_Wo, L0_tok_bo, L0_tok_prelu_a, L0_attn_W_in, L0_attn_b_in, L0_attn_W_conv, L0_attn_b_conv, L0_attn_A_log, L0_attn_W_bc, L0_attn_b_bc, L0_attn_W_dt, L0_attn_b_dt, L0_attn_W_out, L0_attn_b_out, L0_ffn_route_id, L0_ffn_Wi, L0_ffn_bi, L0_ffn_Wr, L0_ffn_br, L0_ffn_Ws, L0_ffn_bs, L0_ffn_Wo, L0_ffn_bo):
    import jax
    import jax.numpy as jnp

    def _L0_tok_ref(x_batched, d_gamma_batched, Wq, bq, Wk, bk, Wv, bv, Wo, bo, prelu_a):
        import jax, jax.numpy as jnp
        import numpy as np
        T, D_IN, D_INT, D_OUT, B = (1024, 64, 64, 64, 8)
        x = x_batched.reshape(x_batched.shape[0], T, D_IN)
        q = x @ Wq + bq
        k = x @ Wk + bk
        v = x @ Wv + bv
        scores = jnp.einsum('btd,bsd->bts', q, k)
        retained = jnp.einsum('bts,bsd->btd', d_gamma_batched * scores, v)
        y = retained @ Wo + bo
        out = jnp.where(y >= 0, y, prelu_a * y)
        return out

    def _L0_attn_ref(x, W_in, b_in, W_conv, b_conv, A_log, W_bc, b_bc, W_dt, b_dt, W_out, b_out):
        import jax, jax.numpy as jnp
        import numpy as np
        B, T, D = (4, 1024, 64)
        EXPAND, D_STATE = (2, 16)
        INNER = D * EXPAND
        x_proj = x @ W_in + b_in
        x_main, x_gate = jnp.split(x_proj, 2, axis=-1)
        x_conv = jax.nn.silu(x_main @ W_conv + b_conv)
        A = -jnp.exp(A_log)
        x_bc = x_conv @ W_bc + b_bc
        B_proj, C_proj = jnp.split(x_bc, 2, axis=-1)
        dt = jax.nn.softplus(x_conv @ W_dt + b_dt)

        def scan_step(h, inputs):
            x_t, dt_t, B_t, C_t = inputs
            A_bar = jnp.exp(dt_t[..., None] * A)
            B_bar = dt_t[..., None] * B_t[:, None, :]
            h_new = A_bar * h + B_bar * x_t[..., None]
            y_t = (h_new * C_t[:, None, :]).sum(axis=-1)
            return (h_new, y_t)
        tm = lambda a: jnp.swapaxes(a, 0, 1)
        h0 = jnp.zeros((x.shape[0], INNER, D_STATE), x_conv.dtype)
        _, y_seq = jax.lax.scan(scan_step, h0, (tm(x_conv), tm(dt), tm(B_proj), tm(C_proj)))
        y = jnp.swapaxes(y_seq, 0, 1)
        y = y * jax.nn.silu(x_gate)
        return y @ W_out + b_out

    def _L0_ffn_ref(x, route_id, Wi, bi, Wr, br, Ws, bs, Wo, bo):
        import jax, jax.numpy as jnp
        import numpy as np
        B, T, IN_DIM = (64, 64, 64)
        HID, OUT_DIM = (128, 64)
        N_LAYERS, N_EXPERTS, N_SHARED = (2, 16, 1)
        flat = x.reshape(-1, x.shape[-1])
        n_tok = flat.shape[0]
        route = jnp.repeat(route_id, n_tok // route_id.shape[0])
        h = jax.nn.relu(flat @ Wi.T + bi)
        n_layers, n_experts = (Wr.shape[0], Wr.shape[1])
        for l in range(n_layers):
            shared = (jnp.einsum('nd,shd->snh', h, Ws[l]) + bs[l][:, None, :]).mean(axis=0)
            routed = jnp.zeros_like(h)
            for e in range(n_experts):
                ye = h @ Wr[l, e].T + br[l, e]
                routed = routed + jnp.where((route == e)[:, None], ye, 0.0)
            h = jax.nn.relu(shared + routed + h)
        out = h @ Wo.T + bo
        return out.reshape(*x.shape[:-1], out.shape[-1])
    h = _L0_tok_ref(x, L0_tok_d_gamma_batched, L0_tok_Wq, L0_tok_bq, L0_tok_Wk, L0_tok_bk, L0_tok_Wv, L0_tok_bv, L0_tok_Wo, L0_tok_bo, L0_tok_prelu_a)
    h = _layernorm(h + _L0_attn_ref(h, L0_attn_W_in, L0_attn_b_in, L0_attn_W_conv, L0_attn_b_conv, L0_attn_A_log, L0_attn_W_bc, L0_attn_b_bc, L0_attn_W_dt, L0_attn_b_dt, L0_attn_W_out, L0_attn_b_out), axis=-1)
    h = _layernorm(h + _L0_ffn_ref(h, L0_ffn_route_id, L0_ffn_Wi, L0_ffn_bi, L0_ffn_Wr, L0_ffn_br, L0_ffn_Ws, L0_ffn_bs, L0_ffn_Wo, L0_ffn_bo), axis=-1)
    return h

_drawn_inputs = setup_inputs


def setup_inputs(seed=0):
    import zlib

    import numpy as np

    out = dict(_drawn_inputs(seed))
    spreads = {'L0_attn_b_in': (0.0, 0.8),
     'L0_attn_b_conv': (0.0, 0.8),
     'L0_attn_b_bc': (0.0, 0.8),
     'L0_attn_b_dt': (0.0, 0.8),
     'L0_attn_b_out': (0.0, 2.0),
     'L0_ffn_bi': (0.0, 0.498),
     'L0_ffn_bo': (0.0, 0.1)}
    factors = {'L0_tok_bo': 8.0,
     'L0_attn_W_in': 4.143,
     'L0_attn_W_conv': 5.052,
     'L0_attn_A_log': 27.121,
     'L0_attn_W_bc': 4.727,
     'L0_attn_W_dt': 8.0,
     'L0_attn_W_out': 4.169,
     'L0_ffn_Wi': 2.729,
     'L0_ffn_Wr': 7.148,
     'L0_ffn_br': 8.0,
     'L0_ffn_Ws': 7.238,
     'L0_ffn_bs': 8.0}
    for name, (base, spread) in spreads.items():
        noise = np.random.default_rng([zlib.crc32(name.encode()), seed]).standard_normal(out[name].shape)
        drawn = base * np.exp(spread * noise) if base else spread * noise
        out[name] = jnp.asarray(drawn.astype(out[name].dtype))
    for name, factor in factors.items():
        out[name] = (out[name] * factor).astype(out[name].dtype)
    return out
```

```python
from contextlib import ExitStack

import concourse.bass as bass
from concourse import mybir

F32 = mybir.dt.float32
BF16 = mybir.dt.bfloat16
I32 = mybir.dt.int32
ALU = mybir.AluOpType
ACT = mybir.ActivationFunctionType
AX = mybir.AxisListType

P = 128
IMAGES = 4
T = 1024
D = 64
INNER = 128
STATES = 16
HID = 128
EXPERTS = 16
LAYERS = 2
HALF = T // 2
TILES = T // P
GROUPS = 64
GROUPS_IMG = GROUPS // IMAGES
GROUP = T // GROUPS_IMG
STEPS = STATES
EPS = 1e-5

USE_Q, USE_K, USE_S = 0, 1, 2
USE_XM, USE_GATE, USE_CONV, USE_BC, USE_DT = 10, 11, 12, 13, 14
WORK_USES = 15
USE_YT, USE_OUT1, USE_H1, USE_F0, USE_L1, USE_L2, USE_OUT2 = 0, 2, 3, 5, 7, 9, 11
TAIL_USES = 12
TAIL_SETUP = 2

PACK = [
    ("wq", 2 * D), ("wk", 2 * D), ("wvb", D + 1), ("wo_tok", D), ("bo_tok", 1), ("prelu_a", 1), ("ident", P),
    ("w_in", 2 * INNER), ("b_in", 2), ("w_conv", INNER), ("b_conv", 1), ("w_bc", 4 * 2 * STATES), ("b_bc", 1),
    ("w_dt", INNER), ("b_dt", 1), ("a_log", STATES), ("w_out", D), ("b_out", D), ("w_i", HID), ("b_i", 1),
    ("w_o", D), ("b_o", D), ("b_r", LAYERS * HID), ("b_s", LAYERS), ("w_s", LAYERS * HID), ("expert", 1),
]
PACK_AT = {}
PACK_COLS = 0
for _name, _cols in PACK:
    PACK_AT[_name] = (PACK_COLS, _cols)
    PACK_COLS += _cols


def vit_layer(nc, xT, gammaT, packed, routed_w, route, out):
    with ExitStack() as ctx:
        def sb(name, shape, dt=F32):
            return ctx.enter_context(nc.sbuf_tensor(name, shape, dt))

        def ps(name, shape):
            return ctx.enter_context(nc.psum_tensor(name, shape, F32))

        def sem(name):
            return ctx.enter_context(nc.semaphore(name))

        pack = sb("pack", [P, PACK_COLS])
        gam = sb("gam", [P, TILES, T])
        expert_w = sb("expert_w", [P, LAYERS, EXPERTS + 1, HID])
        group_w = sb("group_w", [P, GROUPS_IMG, LAYERS, HID])
        sel = sb("sel", [P, STATES, P], BF16)
        wvo = sb("wvo", [P, D])
        neg_a = sb("neg_a", [P, STATES])
        route_i = sb("route_i", [EXPERTS, GROUPS], I32)
        route_f = sb("route_f", [EXPERTS, GROUPS])
        onehot = sb("onehot", [EXPERTS, GROUPS])
        route_ok = sb("route_ok", [1, 2, GROUPS])
        route_x = sb("route_x", [1, GROUPS], I32)
        group_b = sb("group_b", [P, LAYERS, GROUPS])
        ln_s = sb("ln_s", [P, 5, TILES])

        x_in = sb("x_in", [D + 1, T])
        qT = sb("qT", [P, T])
        kT = sb("kT", [P, T])
        xm = kT
        sp_pos = kT
        v_sb = sb("v_sb", [P, TILES, D])
        mixed = sb("mixed", [P, 2, T])
        pre = sb("pre", [P, 2, HALF])
        hT = sb("hT", [P, 2, HALF])
        bc = mixed[:, 0, :]
        xc = mixed[:, 1, :]
        gate = sb("gate", [P, 2, T])
        bc3 = sb("bc3", [P, 2, T], BF16)
        delta = sb("delta", [P, 2, T])
        u = sb("u", [P, 2, T])
        decay = sb("decay", [P, 2, T])
        ub = sb("ub", [P, 2, T])
        h = sb("h", [P, 3, T])
        c_row = sb("c_row", [P, 4, T])
        hc = sb("hc", [P, 2, T])
        y_t = sb("y_t", [P, T])
        h1T = y_t[0:D, :]
        ln_x = sb("ln_x", [P, HALF])
        ln_q = sb("ln_q", [P, HALF])
        h1 = sb("h1", [P, HALF])
        h1b = sb("h1b", [P, HALF])
        f = sb("f", [P, T])
        yg = f
        res = ln_q

        acc_y = ps("acc_y", [P, T])
        b_row = ps("b_row", [P, T])
        work = ps("work", [P, T])
        acc_r = ps("acc_r", [P, HALF])
        tail = ps("tail", [P, HALF])

        c_dram = nc.dram_tensor("c_dram", (IMAGES, STATES, T), F32, kind="Internal").ap()

        def const(name, rows=P, row0=0):
            at, cols = PACK_AT[name]
            return pack[row0:row0 + rows, at:at + cols]

        ident = const("ident")
        w_bc4 = const("w_bc")

        s_pack = sem("pack_loaded")
        s_gam = [sem(f"gamma_loaded_{j}") for j in range(TILES)]
        s_x = sem("x_loaded")
        s_route = sem("route_loaded")
        s_rw = sem("expert_weights_loaded")
        s_ones = sem("ones_row_set")
        s_sel0 = sem("selector_zeroed")
        s_sel = sem("selector_ready")
        s_wvo = sem("wvo_ready")
        s_ea = sem("exp_a_ready")
        s_na = sem("neg_a_ready")
        s_rt = sem("route_steps")
        s_gb = sem("group_bias_ready")
        s_ws = sem("shared_weights_ready")
        s_cw = sem("combined_weights_ready")
        s_gw = [sem(f"group_weights_loaded_{g}") for g in range(2)]

        work_full = sem("work_full")
        work_read = sem("work_read")
        tail_full = sem("tail_full")
        tail_read = sem("tail_read")
        v_full = sem("v_full")
        v_ready = sem("v_ready")
        gv_done = sem("mixed_used")
        prelu_part = sem("prelu_parts")
        h_ready = sem("h_ready")
        conv_ready = sem("conv_ready")
        gate_ready = sem("gate_ready")
        bc_hi = sem("bc_high_ready")
        bc_rest = sem("bc_rest_ready")
        bc_mid = sem("bc_middle_ready")
        bc_rest2 = sem("bc_rest2_ready")
        bc_split = sem("bc_split_ready")
        c_stored = sem("c_stored")
        sp_step = sem("softplus_steps")
        delta_ready = sem("delta_ready")
        u_ready = sem("u_ready")

        b_ready = sem("b_row_ready")
        decay_ready = sem("decay_ready")
        ub_ready = sem("ub_ready")
        scan_done = sem("scan_done")
        c_loaded = [sem(f"c_row_loaded_{i}") for i in range(4)]
        hc_ready = sem("hc_ready")
        hc_used = sem("hc_used")
        y_read = sem("y_read")

        ln_sum = sem("ln_sum")
        ln_cent = sem("ln_centred")
        ln_sq = sem("ln_squared")
        ln_var = sem("ln_variance")
        ln_std = sem("ln_variance_eps")
        ln_log = sem("ln_log_steps")
        ln_pow = sem("ln_scale_ready")
        ln_out = sem("ln_out")
        h1b_ready = sem("h1_with_bias")
        relu_done = sem("relu_done")
        stored = sem("out_stored")

        PHASES = range(-1, IMAGES + 1)

        def step_of(p, n):
            head = p + 1 if p + 1 < IMAGES else None
            scan = p if 0 <= p < IMAGES else None
            last = p - 1 if p >= 1 else None
            return head, scan, last, STEPS * p + n

        def work_use(image, use):
            return WORK_USES * image + use

        def tail_use(image, use):
            return TAIL_SETUP + TAIL_USES * image + use

        def bcast(ap, shape):
            return ap.unsqueeze(2).broadcast_to(shape)

        block = ctx.enter_context(nc.Block())

        @block.sync
        def _(sp):
            sp.dma_start(x_in[0:D, :], xT[0]).then_inc(s_x, 16)
            sp.dma_start(gam[:, 0, :], gammaT[0:P, :]).then_inc(s_gam[0], 16)
            for j in range(1, TILES):
                sp.dma_start(gam[:, j, :], gammaT[j * P:(j + 1) * P, :]).then_inc(s_gam[j], 16)
            sp.dma_start(expert_w[:, :, 0:EXPERTS, :], routed_w).then_inc(s_rw, 16)

            def load_c(k):
                b, n = k // STEPS, k % STEPS
                if n == 0:
                    sp.wait_ge(c_stored, 16 * (b + 1))
                if k >= 4:
                    sp.wait_ge(hc_ready, k - 3)
                sp.dma_start(c_row[:, k % 4, :], c_dram[b, n, :].partition_broadcast(P)).then_inc(c_loaded[k % 4], 16)

            def load_group(b, g):
                if b >= 1:
                    sp.wait_ge(tail_full, tail_use(b - 1, USE_L2 + g // 8) + 1)
                e = sp.value_load(route_x[0:1, GROUPS_IMG * b + g:GROUPS_IMG * b + g + 1],
                                  min_val=0, max_val=EXPERTS)
                sp.dma_start(group_w[:, g, :, :].unsqueeze(2), expert_w[:, :, bass.ds(e, 1), :])\
                    .then_inc(s_gw[g // 8], 16)

            for p in PHASES:
                for n in range(STEPS):
                    head, scan, last, k = step_of(p, n)
                    if head is not None and n == 3 and head + 1 < IMAGES:
                        sp.wait_ge(work_full, work_use(head, USE_K) + 1)
                        sp.wait_ge(v_full, head + 1)
                        sp.dma_start(x_in[0:D, :], xT[head + 1]).then_inc(s_x, 16)
                    if head is not None and n == 14:
                        sp.wait_ge(work_read, work_use(head, USE_BC) + 1)
                        sp.dma_start(c_dram[head], mixed[STATES:2 * STATES, 0, :]).then_inc(c_stored, 16)
                    for ahead in {13: (), 14: (k + 2, k + 3)}.get(n, (k + 3,)):
                        if 0 <= ahead < STEPS * IMAGES:
                            load_c(ahead)
                    if last is not None and n < 8:
                        if last == 0 and n == 0:
                            sp.wait_ge(s_rt, 5)
                            sp.wait_ge(s_cw, 3)
                        load_group(last, 2 * n)
                        load_group(last, 2 * n + 1)
                    if last is not None and n == 15:
                        sp.wait_ge(ln_out, 2 * last + 2)
                        sp.dma_start(out[last].rearrange("(c t) d -> t c d", t=P),
                                     res[:, :].rearrange("p (c d) -> p c d", d=D)).then_inc(stored, 16)
            sp.wait_ge(stored, 16 * IMAGES)

        @block.tensor
        def _(pe):
            pe.wait_ge(s_pack, 16)
            nc.tensor.matmul(tail[0:D + 1, 0:D], const("wvb", D), const("wo_tok", D), start=True, stop=True)\
                .then_inc(tail_full, 1)

            def begin_work(image, use):
                if work_use(image, use):
                    pe.wait_ge(work_read, work_use(image, use))

            def begin_tail(image, use):
                pe.wait_ge(tail_read, tail_use(image, use))

            def project(weights, moving, lo):
                for i in range(2):
                    mm = nc.tensor.matmul(work[:, i * HALF:(i + 1) * HALF], weights(i), moving(i), start=True, stop=True)
                return mm

            def states_in(k):
                b, n = k // STEPS, k % STEPS
                if n == 0:
                    pe.wait_ge(bc_split, b + 1)
                    if b == 0:
                        pe.wait_ge(s_sel, 1)
                if k:
                    pe.wait_ge(ub_ready, k)
                for i in range(2):
                    mm = nc.tensor.matmul(b_row[:, i * HALF:(i + 1) * HALF], sel[:, n, :],
                                          bc3[:, b % 2, i * HALF:(i + 1) * HALF], start=True, stop=True)
                mm.then_inc(b_ready, 1)

            def states_out(k):
                b, n = k // STEPS, k % STEPS
                pe.wait_ge(hc_ready, k + 1)
                if n == 0 and b:
                    pe.wait_ge(y_read, b)
                for c in range(TILES):
                    mm = nc.tensor.matmul(acc_y[:, c * P:(c + 1) * P], hc[:, k % 2, c * P:(c + 1) * P], ident,
                                          start=(n == 0 and c % 4 == 0), stop=(n == STATES - 1), is_transpose=True,
                                          skip_group_check=True)
                mm.then_inc(hc_used, 1)

            def head_part(b, n):
                if n == 0:
                    pe.wait_ge(s_x, 16 * (b + 1))
                    if b == 0:
                        pe.wait_ge(s_ones, 1)
                        pe.wait_ge(s_wvo, 1)
                    begin_work(b, USE_Q)
                    project(lambda i: const("wq", D + 1), lambda i: x_in[:, i * HALF:(i + 1) * HALF], 0)\
                        .then_inc(work_full, 1)
                    if b:
                        pe.wait_ge(prelu_part, 2 * b)
                    for c in range(TILES):
                        mm = nc.tensor.matmul(acc_r[:, c * D:(c + 1) * D], x_in[:, c * P:(c + 1) * P],
                                              wvo[0:D + 1, :], start=True, stop=True)
                    mm.then_inc(v_full, 1)
                    begin_work(b, USE_K)
                    project(lambda i: const("wk", D + 1), lambda i: x_in[:, i * HALF:(i + 1) * HALF], 0)\
                        .then_inc(work_full, 1)
                if 2 <= n < 2 + TILES:
                    j = n - 2
                    lo = D * (j % 2)
                    begin_work(b, USE_S + j)
                    for i in range(2):
                        mm = nc.tensor.matmul(work[:, i * HALF:(i + 1) * HALF], kT[lo:lo + D, j * P:(j + 1) * P],
                                              qT[lo:lo + D, i * HALF:(i + 1) * HALF], start=True, stop=True)
                    mm.then_inc(work_full, 1)
                if 3 <= n < 3 + TILES:
                    j = n - 3
                    pe.wait_ge(work_read, work_use(b, USE_S + j) + 1)
                    if j == 0:
                        pe.wait_ge(v_ready, b + 1)
                    for i in range(2):
                        mm = nc.tensor.matmul(acc_r[D * i:D * i + D, :], v_sb[:, j, :],
                                              mixed[:, j % 2, i * HALF:(i + 1) * HALF],
                                              start=(j == 0), stop=(j == TILES - 1), skip_group_check=True)
                    mm.then_inc(gv_done, 1)
                if n == 11:
                    pe.wait_ge(h_ready, b + 1)
                    for use, at in ((USE_XM, 0), (USE_GATE, INNER)):
                        begin_work(b, use)
                        for i in range(2):
                            mm = nc.tensor.matmul(work[:, i * HALF:(i + 1) * HALF],
                                                  const("w_in", D, D * i)[:, at:at + INNER],
                                                  hT[D * i:D * i + D, b % 2, :], start=True, stop=True)
                        mm.then_inc(work_full, 1)
                if n == 12:
                    begin_work(b, USE_CONV)
                    project(lambda i: const("w_conv"), lambda i: xm[:, i * HALF:(i + 1) * HALF], 0)\
                        .then_inc(work_full, 1)
                if n == 13:
                    for use, name in ((USE_BC, "w_bc"), (USE_DT, "w_dt")):
                        begin_work(b, use)
                        pe.wait_ge(conv_ready, b + 1)
                        project(lambda i: const(name), lambda i: xc[:, i * HALF:(i + 1) * HALF], 0)\
                            .then_inc(work_full, 1)

            def last_part(b, n):
                if n == 2:
                    for i in range(2):
                        begin_tail(b, USE_YT + i)
                        if i == 0:
                            pe.wait_ge(y_read, b + 1)
                        for c in range(4 * i, 4 * i + 4):
                            mm = nc.tensor.transpose(tail[:, (c % 4) * P:(c % 4 + 1) * P], y_t[:, c * P:(c + 1) * P], ident)
                        mm.then_inc(tail_full, 1)
                if n == 3:
                    begin_tail(b, USE_OUT1)
                    for c in range(TILES):
                        lo, at = D * (c // 4), (c % 4) * P
                        nc.tensor.matmul(tail[:, c * D:(c + 1) * D], yg[:, c * P:(c + 1) * P], const("w_out"),
                                         start=True, stop=False)
                        mm = nc.tensor.matmul(tail[:, c * D:(c + 1) * D], hT[:, b % 2, at:at + P],
                                              ident[:, lo:lo + D], start=False, stop=True)
                    mm.then_inc(tail_full, 1)
                if n == 8:
                    for i in range(2):
                        begin_tail(b, USE_H1 + i)
                        pe.wait_ge(ln_out, 2 * b + 1)
                        for c in range(4 * i, 4 * i + 4):
                            mm = nc.tensor.transpose(tail[0:D, (c % 4) * P:(c % 4 + 1) * P], h1[:, c * D:(c + 1) * D], ident)
                        mm.then_inc(tail_full, 1)
                if n == 9:
                    for i in range(2):
                        begin_tail(b, USE_F0 + i)
                        nc.tensor.matmul(tail[:, :], const("w_i", D), h1T[:, i * HALF:(i + 1) * HALF],
                                         start=True, stop=True).then_inc(tail_full, 1)
                if n in (10, 11):
                    layer = n - 10
                    for i in range(2):
                        begin_tail(b, (USE_L1, USE_L2)[layer] + i)
                        if layer == 0:
                            pe.wait_ge(s_gw[i], 16 * 8 * (b + 1))
                        else:
                            pe.wait_ge(relu_done, 4 * b + i + 1)
                        for g in range(8 * i, 8 * i + 8):
                            mm = nc.tensor.matmul(tail[:, (g % 8) * GROUP:(g % 8 + 1) * GROUP], group_w[:, g, layer, :],
                                                  f[:, g * GROUP:(g + 1) * GROUP], start=True, stop=True)
                        mm.then_inc(tail_full, 1)
                if n == 12:
                    begin_tail(b, USE_OUT2)
                    pe.wait_ge(relu_done, 4 * b + 4)
                    for c in range(TILES):
                        mm = nc.tensor.matmul(tail[:, c * D:(c + 1) * D], f[:, c * P:(c + 1) * P], const("w_o"),
                                              start=True, stop=True)
                    mm.then_inc(tail_full, 1)

            for p in PHASES:
                for n in range(STEPS):
                    head, scan, last, k = step_of(p, n)
                    if scan is not None:
                        states_in(k)
                    if 0 <= k - 2 < STEPS * IMAGES:
                        states_out(k - 2)
                    if head is not None:
                        head_part(head, n)
                    if last is not None:
                        last_part(last, n)
                    if p == -1 and n == 13:
                        pe.wait_ge(s_rt, 2)
                        pe.wait_ge(tail_read, 1)
                        for layer in range(LAYERS):
                            mm = nc.tensor.matmul(tail[:, layer * GROUPS:(layer + 1) * GROUPS],
                                                  const("b_r", EXPERTS)[:, layer * HID:(layer + 1) * HID],
                                                  onehot[:, :], start=True, stop=True)
                        mm.then_inc(tail_full, 1)

        @block.scalar
        def _(act):
            act.dma_start(pack[:, :], packed).then_inc(s_pack, 16)
            act.dma_start(route_i[:, :], route.partition_broadcast(EXPERTS)).then_inc(s_route, 16)
            act.wait_ge(s_pack, 16)
            nc.scalar.activation(neg_a[:, :], const("a_log"), ACT.Exp).then_inc(s_ea, 1)

            def decay_of(k):
                b, n = k // STEPS, k % STEPS
                if n == 0:
                    act.wait_ge(delta_ready, b + 1)
                    if b == 0:
                        act.wait_ge(s_na, 1)
                if k >= 2:
                    act.wait_ge(scan_done, k - 1)
                nc.scalar.activation(decay[:, k % 2, :], delta[:, b % 2, :], ACT.Exp, scale=neg_a[:, n:n + 1])\
                    .then_inc(decay_ready, 1)

            def head_part(b, n):
                if n == 0:
                    act.wait_ge(work_full, work_use(b, USE_Q) + 1)
                    nc.scalar.activation(qT[:, :], work[:, :], ACT.Copy).then_inc(work_read, 1)
                    act.wait_ge(v_full, b + 1)
                    nc.scalar.activation(v_sb[:, :, :], acc_r[:, :].rearrange("p (c d) -> p c d", d=D), ACT.Copy)\
                        .then_inc(v_ready, 1)
                    act.wait_ge(work_full, work_use(b, USE_K) + 1)
                    nc.scalar.activation(kT[:, :], work[:, :], ACT.Copy).then_inc(work_read, 1)
                if n == 11:
                    act.wait_ge(work_full, work_use(b, USE_XM) + 1)
                    nc.scalar.activation(xm[:, :], work[:, :], ACT.Identity, bias=const("b_in")[:, 0:1])\
                        .then_inc(work_read, 1)
                    act.wait_ge(work_full, work_use(b, USE_GATE) + 1)
                    if b >= 2:
                        act.wait_ge(tail_read, tail_use(b - 2, USE_YT + 1) + 1)
                    nc.scalar.activation(gate[:, b % 2, :], work[:, :], ACT.Identity, bias=const("b_in")[:, 1:2])\
                        .then_inc(work_read, 1)
                if n == 12:
                    act.wait_ge(work_full, work_use(b, USE_CONV) + 1)
                    if b:
                        act.wait_ge(u_ready, b)
                    nc.scalar.activation(xc, work[:, :], ACT.Silu, bias=const("b_conv")).then_inc(conv_ready, 1)
                    act.wait_ge(conv_ready, b + 1)
                    act.sem_inc(work_read, 1)
                    nc.scalar.activation(gate[:, b % 2, :], gate[:, b % 2, :], ACT.Silu).then_inc(gate_ready, 1)
                if n == 13:
                    act.wait_ge(work_full, work_use(b, USE_BC) + 1)
                    if b:
                        act.wait_ge(c_stored, 16 * b)
                    nc.scalar.activation(bc, work[:, :], ACT.Identity, bias=const("b_bc")).then_inc(work_read, 1)
                    act.wait_ge(work_full, work_use(b, USE_DT) + 1)
                    if b >= 2:
                        act.wait_ge(decay_ready, STEPS * (b - 1))
                    nc.scalar.activation(delta[:, b % 2, :], work[:, :], ACT.Abs, bias=const("b_dt")).then_inc(sp_step, 1)
                    nc.scalar.activation(sp_pos[:, :], work[:, :], ACT.Relu, bias=const("b_dt")).then_inc(work_read, 1)
                    act.wait_ge(sp_step, 3 * b + 1)
                    nc.scalar.activation(delta[:, b % 2, :], delta[:, b % 2, :], ACT.Exp, scale=-1.0).then_inc(sp_step, 1)
                    act.wait_ge(work_read, work_use(b, USE_DT) + 1)
                    if b >= 2:
                        act.wait_ge(b_ready, STEPS * (b - 1))
                    nc.scalar.activation(bc3[:, b % 2, :], bc, ACT.Copy).then_inc(bc_hi, 1)
                    act.wait_ge(sp_step, 3 * b + 2)
                    nc.scalar.activation(delta[:, b % 2, :], delta[:, b % 2, :], ACT.Ln, bias=1.0).then_inc(sp_step, 1)
                if n == 14:
                    act.wait_ge(bc_rest, b + 1)
                    nc.scalar.activation(bc3[D:P, b % 2, :], qT[D:P, :], ACT.Copy).then_inc(bc_mid, 1)
                    act.wait_ge(bc_rest2, b + 1)
                    nc.scalar.activation(bc3[96:P, b % 2, :], qT[96:P, :], ACT.Copy).then_inc(bc_split, 1)

            def last_part(b, n):
                if n == 1:
                    act.wait_ge(hc_used, STEPS * (b + 1))
                    nc.scalar.activation(y_t[:, :], acc_y[:, :], ACT.Copy).then_inc(y_read, 1)
                if n in (6, 14):
                    count = 2 * b + (n == 14)
                    act.wait_ge(ln_std, count + 1)
                    nc.scalar.activation(ln_s[:, 3, :], ln_s[:, 2, :], ACT.Ln).then_inc(ln_log, 1)
                    act.wait_ge(ln_log, 2 * count + 1)
                    nc.scalar.activation(ln_s[:, 3, :], ln_s[:, 3, :], ACT.Exp, scale=-0.5).then_inc(ln_log, 1)
                if n == 8:
                    for i in range(2):
                        act.wait_ge(tail_full, tail_use(b, USE_H1 + i) + 1)
                        nc.scalar.activation(h1T[:, i * HALF:(i + 1) * HALF], tail[0:D, :], ACT.Copy)\
                            .then_inc(tail_read, 1)
                if n == 9:
                    for i in range(2):
                        act.wait_ge(tail_full, tail_use(b, USE_F0 + i) + 1)
                        nc.scalar.activation(f[:, i * HALF:(i + 1) * HALF], tail[:, :], ACT.Relu, bias=const("b_i"))\
                            .then_inc(tail_read, 1)
                if n in (10, 11):
                    layer = n - 10
                    for i in range(2):
                        act.wait_ge(tail_read, tail_use(b, (USE_L1, USE_L2)[layer] + i) + 1)
                        nc.scalar.activation(f[:, i * HALF:(i + 1) * HALF], f[:, i * HALF:(i + 1) * HALF], ACT.Relu)\
                            .then_inc(relu_done, 1)

            for p in PHASES:
                for n in range(STEPS):
                    head, scan, last, k = step_of(p, n)
                    if scan is not None:
                        decay_of(k)
                    if head is not None:
                        head_part(head, n)
                    if last is not None:
                        last_part(last, n)

        @block.gpsimd
        def _(pool):
            nc.gpsimd.memset(sel[:, :, :], 0.0).then_inc(s_sel0, 1)
            for i, lo in enumerate((0, 64, 96)):
                pool.wait_ge(s_sel0, i + 1)
                nc.gpsimd.affine_select(out=sel[:, :, :], in_=sel[:, :, :], compare_op=ALU.not_equal, fill=1.0,
                                        base=-lo, pattern=[[-1, STATES], [0, P]], channel_multiplier=1)\
                    .then_inc(s_sel if lo == 96 else s_sel0, 1)

            def combine_weights():
                pool.wait_ge(s_pack, 16)
                for layer in range(LAYERS):
                    at = PACK_AT["w_s"][0] + layer * HID
                    nc.gpsimd.tensor_tensor(expert_w[:, layer, EXPERTS, :], pack[:, at:at + HID], ident, ALU.add)\
                        .then_inc(s_ws, 1)
                pool.wait_ge(s_ws, 2)
                pool.wait_ge(s_rw, 16)
                for layer in range(LAYERS):
                    w = expert_w[:, layer, 0:EXPERTS, :]
                    nc.gpsimd.tensor_tensor(w, w, expert_w[:, layer, EXPERTS, :].unsqueeze(1)
                                            .broadcast_to([P, EXPERTS, HID]), ALU.add).then_inc(s_cw, 1)
                pool.wait_ge(s_cw, 2)
                pool.sem_inc(s_cw, 1)

            def weigh(k):
                pool.wait_ge(scan_done, k + 1)
                pool.wait_ge(c_loaded[k % 4], 16 * (k // 4 + 1))
                if k >= 2:
                    pool.wait_ge(hc_used, k - 1)
                nc.gpsimd.tensor_tensor(hc[:, k % 2, :], h[:, k % 3, :], c_row[:, k % 4, :], ALU.mult)\
                    .then_inc(hc_ready, 1)

            def head_part(b, n):
                if n == 13:
                    pool.wait_ge(bc_hi, b + 1)
                    nc.gpsimd.tensor_tensor(qT[:, :], bc, bc3[:, b % 2, :], ALU.subtract).then_inc(bc_rest, 1)
                if n == 14:
                    pool.wait_ge(sp_step, 3 * b + 3)
                    nc.gpsimd.tensor_tensor(delta[:, b % 2, :], delta[:, b % 2, :], sp_pos[:, :], ALU.add)\
                        .then_inc(delta_ready, 1)
                    pool.wait_ge(bc_mid, b + 1)
                    nc.gpsimd.tensor_tensor(qT[:, :], qT[:, :], bc3[:, b % 2, :], ALU.subtract)\
                        .then_inc(bc_rest2, 1)
                    pool.wait_ge(delta_ready, b + 1)
                    if b >= 2:
                        pool.wait_ge(ub_ready, STEPS * (b - 1))
                    nc.gpsimd.tensor_tensor(u[:, b % 2, :], delta[:, b % 2, :], xc, ALU.mult).then_inc(u_ready, 1)

            def last_part(b, n):
                if n == 4:
                    pool.wait_ge(ln_cent, 2 * b + 1)
                    if b:
                        pool.wait_ge(stored, 16 * b)
                    nc.gpsimd.tensor_tensor(ln_q[:, :], ln_x[:, :], ln_x[:, :], ALU.mult).then_inc(ln_sq, 1)
                if n == 8:
                    pool.wait_ge(ln_out, 2 * b + 1)
                    if b:
                        pool.wait_ge(tail_read, tail_use(b - 1, USE_OUT2) + 1)
                    nc.gpsimd.tensor_tensor(h1b[:, :].rearrange("p (c d) -> p c d", d=D),
                                            h1[:, :].rearrange("p (c d) -> p c d", d=D),
                                            const("b_o").unsqueeze(1).broadcast_to([P, TILES, D]), ALU.add)\
                        .then_inc(h1b_ready, 1)
                if n == 13:
                    pool.wait_ge(ln_cent, 2 * b + 2)
                    if b:
                        pool.wait_ge(stored, 16 * b)
                    nc.gpsimd.tensor_tensor(ln_q[:, :], ln_x[:, :], ln_x[:, :], ALU.mult).then_inc(ln_sq, 1)
                if n in (6, 14):
                    count = 2 * b + (n == 14)
                    v, r, t = ln_s[:, 2, :], ln_s[:, 3, :], ln_s[:, 4, :]
                    pool.wait_ge(ln_log, 2 * count + 2)
                    nc.gpsimd.tensor_tensor(t, r, r, ALU.mult).then_inc(ln_pow, 1)
                    pool.wait_ge(ln_pow, 4 * count + 1)
                    nc.gpsimd.tensor_tensor(t, t, v, ALU.mult).then_inc(ln_pow, 1)
                    pool.wait_ge(ln_pow, 4 * count + 2)
                    nc.gpsimd.tensor_scalar(t, t, -0.5, 1.5, ALU.mult, ALU.add).then_inc(ln_pow, 1)
                    pool.wait_ge(ln_pow, 4 * count + 3)
                    nc.gpsimd.tensor_tensor(r, r, t, ALU.mult).then_inc(ln_pow, 1)

            for p in PHASES:
                for n in range(STEPS):
                    head, scan, last, k = step_of(p, n)
                    if 0 <= k - 1 < STEPS * IMAGES:
                        weigh(k - 1)
                    if head is not None:
                        head_part(head, n)
                    if last is not None:
                        last_part(last, n)
                    if p == -1 and n == 10:
                        combine_weights()

        @block.vector
        def _(dve):
            nc.vector.memset(x_in[D:D + 1, :], 1.0).then_inc(s_ones, 1)
            dve.wait_ge(tail_full, 1)
            nc.vector.tensor_copy(wvo[0:D + 1, :], tail[0:D + 1, 0:D]).then_inc(s_wvo, 1)
            dve.wait_ge(s_wvo, 1)
            dve.sem_inc(tail_read, 1)
            dve.wait_ge(s_ea, 1)
            nc.vector.tensor_scalar(neg_a[:, :], neg_a[:, :], -1.0, None, ALU.mult).then_inc(s_na, 1)

            def routes():
                dve.wait_ge(s_route, 16)
                dve.wait_ge(s_pack, 16)
                nc.vector.tensor_copy(route_f[:, :], route_i[:, :]).then_inc(s_rt, 1)
                dve.wait_ge(s_rt, 1)
                nc.vector.tensor_scalar(onehot[:, :], route_f[:, :], const("expert", EXPERTS), None, ALU.is_equal)\
                    .then_inc(s_rt, 1)
                nc.vector.tensor_scalar(route_ok[:, 0, :], route_f[0:1, :], 0.0, None, ALU.is_ge).then_inc(s_rt, 1)
                dve.wait_ge(s_rt, 3)
                nc.vector.scalar_tensor_tensor(out=route_ok[:, 1, :], in0=route_f[0:1, :], scalar=float(EXPERTS - 1),
                                               in1=route_ok[:, 0, :], op0=ALU.is_le, op1=ALU.mult).then_inc(s_rt, 1)
                dve.wait_ge(s_rt, 4)
                nc.vector.scalar_tensor_tensor(out=route_ok[:, 0, :], in0=route_f[0:1, :], scalar=float(EXPERTS),
                                               in1=route_ok[:, 1, :], op0=ALU.subtract, op1=ALU.mult)\
                    .then_inc(s_gb, 1)
                dve.wait_ge(s_gb, 1)
                nc.vector.tensor_scalar(route_x[:, :], route_ok[:, 0, :], float(EXPERTS), None, ALU.add)\
                    .then_inc(s_rt, 1)

            def group_bias():
                dve.wait_ge(tail_full, 2)
                for layer in range(LAYERS):
                    at = PACK_AT["b_s"][0] + layer
                    op = nc.vector.tensor_scalar(group_b[:, layer, :], tail[:, layer * GROUPS:(layer + 1) * GROUPS],
                                                 pack[:, at:at + 1], None, ALU.add)
                op.then_inc(tail_read, 1)

            def drive(k):
                b, n = k // STEPS, k % STEPS
                if n == 0:
                    dve.wait_ge(u_ready, b + 1)
                dve.wait_ge(b_ready, k + 1)
                if k >= 2:
                    dve.wait_ge(scan_done, k - 1)
                nc.vector.tensor_tensor(ub[:, k % 2, :], u[:, b % 2, :], b_row[:, :], ALU.mult).then_inc(ub_ready, 1)

            def scan_step(k):
                dve.wait_ge(ub_ready, k + 1)
                dve.wait_ge(decay_ready, k + 1)
                if k >= 3:
                    dve.wait_ge(hc_ready, k - 2)
                nc.vector.tensor_tensor_scan(h[:, k % 3, :], decay[:, k % 2, :], ub[:, k % 2, :], 0.0,
                                             ALU.mult, ALU.add).then_inc(scan_done, 1)

            def head_part(b, n):
                if 2 <= n < 2 + TILES:
                    j = n - 2
                    if b == 0:
                        dve.wait_ge(s_gam[j], 16)
                    dve.wait_ge(work_full, work_use(b, USE_S + j) + 1)
                    if b and j < 2:
                        dve.wait_ge(*((bc_rest, b), (u_ready, b))[j])
                        dve.wait_ge(c_stored, 16 * b)
                    if TILES * b + j >= 2:
                        dve.wait_ge(gv_done, TILES * b + j - 1)
                    nc.vector.tensor_tensor(mixed[:, j % 2, :], gam[:, j, :], work[:, :], ALU.mult)\
                        .then_inc(work_read, 1)
                if n == 10:
                    dve.wait_ge(gv_done, TILES * (b + 1))
                    for i, op in enumerate((ALU.min, ALU.max)):
                        nc.vector.tensor_scalar(pre[:, i, :], acc_r[:, :], const("bo_tok"), 0.0, ALU.add, op)\
                            .then_inc(prelu_part, 1)
                    dve.wait_ge(prelu_part, 2 * b + 2)
                    if b >= 2:
                        dve.wait_ge(tail_full, tail_use(b - 2, USE_OUT1) + 1)
                    nc.vector.scalar_tensor_tensor(out=hT[:, b % 2, :], in0=pre[:, 0, :], scalar=const("prelu_a"),
                                                   in1=pre[:, 1, :], op0=ALU.mult, op1=ALU.add).then_inc(h_ready, 1)

            def rows(ap):
                return ap.rearrange("p (c d) -> p c d", d=D)

            def norm(count, part, dst):
                x3 = rows(ln_x[:, :])
                if part == 0:
                    nc.vector.tensor_reduce(ln_s[:, 0, :], x3, AX.X, ALU.add).then_inc(ln_sum, 1)
                    dve.wait_ge(ln_sum, count + 1)
                    nc.vector.scalar_tensor_tensor(out=x3, in0=bcast(ln_s[:, 0, :], [P, TILES, D]), scalar=-1.0 / D,
                                                   in1=x3, op0=ALU.mult, op1=ALU.add).then_inc(ln_cent, 1)
                if part == 1:
                    dve.wait_ge(ln_sq, count + 1)
                    nc.vector.tensor_reduce(ln_s[:, 1, :], rows(ln_q[:, :]), AX.X, ALU.add).then_inc(ln_var, 1)
                    dve.wait_ge(ln_var, count + 1)
                    nc.vector.tensor_scalar(ln_s[:, 2, :], ln_s[:, 1, :], 1.0 / D, EPS, ALU.mult, ALU.add)\
                        .then_inc(ln_std, 1)
                if part == 2:
                    dve.wait_ge(ln_pow, 4 * (count + 1))
                    nc.vector.tensor_tensor(dst, x3, bcast(ln_s[:, 3, :], [P, TILES, D]), ALU.mult).then_inc(ln_out, 1)

            def last_part(b, n):
                if n == 2:
                    for i in range(2):
                        dve.wait_ge(tail_full, tail_use(b, USE_YT + i) + 1)
                        if i == 0:
                            dve.wait_ge(gate_ready, b + 1)
                        nc.vector.tensor_tensor(yg[:, i * HALF:(i + 1) * HALF], gate[:, b % 2, i * HALF:(i + 1) * HALF],
                                                tail[:, :], ALU.mult).then_inc(tail_read, 1)
                if n == 3:
                    dve.wait_ge(tail_full, tail_use(b, USE_OUT1) + 1)
                    nc.vector.tensor_tensor(rows(ln_x[:, :]), rows(tail[:, :]),
                                            const("b_out").unsqueeze(1).broadcast_to([P, TILES, D]), ALU.add)\
                        .then_inc(tail_read, 1)
                    dve.wait_ge(tail_read, tail_use(b, USE_OUT1) + 1)
                    norm(2 * b, 0, None)
                if n == 6:
                    norm(2 * b, 1, None)
                if n == 7:
                    if b:
                        dve.wait_ge(h1b_ready, b)
                    norm(2 * b, 2, rows(h1[:, :]))
                if n in (10, 11):
                    layer = n - 10
                    for i in range(2):
                        dve.wait_ge(tail_full, tail_use(b, (USE_L1, USE_L2)[layer] + i) + 1)
                        g0 = GROUPS_IMG * b + 8 * i
                        nc.vector.tensor_tensor(
                            f[:, i * HALF:(i + 1) * HALF].rearrange("p (g t) -> p g t", t=GROUP),
                            tail[:, :].rearrange("p (g t) -> p g t", t=GROUP),
                            bcast(group_b[:, layer, g0:g0 + 8], [P, 8, GROUP]), ALU.add).then_inc(tail_read, 1)
                if n == 12:
                    dve.wait_ge(tail_full, tail_use(b, USE_OUT2) + 1)
                    dve.wait_ge(h1b_ready, b + 1)
                    nc.vector.tensor_tensor(ln_x[:, :], tail[:, :], h1b[:, :], ALU.add).then_inc(tail_read, 1)
                    dve.wait_ge(tail_read, tail_use(b, USE_OUT2) + 1)
                    norm(2 * b + 1, 0, None)
                if n == 14:
                    norm(2 * b + 1, 1, None)
                if n == 15:
                    norm(2 * b + 1, 2, rows(res[:, :]))

            for p in PHASES:
                for n in range(STEPS):
                    head, scan, last, k = step_of(p, n)
                    if scan is not None:
                        drive(k)
                    if 0 <= k - 1 < STEPS * IMAGES:
                        scan_step(k - 1)
                    if head is not None:
                        head_part(head, n)
                    if last is not None:
                        last_part(last, n)
                    if p == -1 and n == 1:
                        routes()
                    if p == -1 and n == 13:
                        group_bias()


def kernel(**inputs):
    import numpy as np
    import concourse.bacc as bacc
    from concourse.bass_utils import run_bass_kernel_spmd

    a = {name: np.ascontiguousarray(value) for name, value in inputs.items()}
    tok = {n[len("L0_tok_"):]: v for n, v in a.items() if n.startswith("L0_tok_")}
    att = {n[len("L0_attn_"):]: v for n, v in a.items() if n.startswith("L0_attn_")}
    ffn = {n[len("L0_ffn_"):]: v for n, v in a.items() if n.startswith("L0_ffn_")}

    packed = np.zeros((P, PACK_COLS), np.float32)

    def place(name, value, row0=0, col0=0):
        at = PACK_AT[name][0] + col0
        packed[row0:row0 + value.shape[0], at:at + value.shape[1]] = value

    for i in range(2):
        for name, w, b in (("wq", tok["Wq"], tok["bq"]), ("wk", tok["Wk"], tok["bk"])):
            place(name, w, 0, D * i)
            place(name, b[None, :], D, D * i)
        place("bo_tok", tok["bo"][:, None], D * i)
        place("w_in", att["W_in"], D * i)
        place("b_in", att["b_in"][INNER * i:INNER * (i + 1), None], 0, i)
    place("wvb", tok["Wv"].T)
    place("wvb", tok["bv"][:, None], 0, D)
    place("wo_tok", tok["Wo"])
    place("prelu_a", np.broadcast_to(tok["prelu_a"].reshape(1, 1), (P, 1)))
    place("ident", np.eye(P, dtype=np.float32))
    place("w_conv", att["W_conv"])
    place("b_conv", att["b_conv"][:, None])
    for i in range(4):
        place("w_bc", att["W_bc"], 0, 2 * STATES * i)
        place("b_bc", att["b_bc"][:, None], 2 * STATES * i)
    place("w_dt", att["W_dt"])
    place("b_dt", att["b_dt"][:, None])
    place("a_log", att["A_log"])
    place("w_out", att["W_out"])
    place("b_out", np.broadcast_to(att["b_out"], (P, D)))
    place("w_i", ffn["Wi"].T)
    place("b_i", ffn["bi"][:, None])
    place("w_o", ffn["Wo"].T)
    place("b_o", np.broadcast_to(ffn["bo"], (P, D)))
    for layer in range(LAYERS):
        place("b_r", ffn["br"][layer], 0, HID * layer)
        place("b_s", ffn["bs"][layer, 0][:, None], 0, layer)
        place("w_s", ffn["Ws"][layer, 0].T, 0, HID * layer)
    place("expert", np.arange(EXPERTS, dtype=np.float32)[:, None])

    arrays = {
        "xT": np.ascontiguousarray(a["x"].reshape(IMAGES, T, D).transpose(0, 2, 1)),
        "gammaT": np.ascontiguousarray(tok["d_gamma_batched"].T),
        "packed": packed,
        "routed_w": np.ascontiguousarray(ffn["Wr"].transpose(3, 0, 1, 2)),
        "route": ffn["route_id"],
    }
    nc = bacc.Bacc("TRN2", target_bir_lowering=False, num_devices=1)
    args = [nc.dram_tensor(name, v.shape, mybir.dt.from_np(v.dtype), kind="ExternalInput").ap()
            for name, v in arrays.items()]
    out = nc.dram_tensor("out", (IMAGES, T, D), F32, kind="ExternalOutput").ap()
    vit_layer(nc, *args, out)
    result = run_bass_kernel_spmd(nc, [arrays], core_ids=[0])
    return result.results[0]["out"]
```

```python
from contextlib import ExitStack

import concourse.bass as bass
from concourse import mybir

F32 = mybir.dt.float32
BF16 = mybir.dt.bfloat16
I32 = mybir.dt.int32
ALU = mybir.AluOpType
ACT = mybir.ActivationFunctionType
AX = mybir.AxisListType

P = 128
IMAGES = 4
T = 1024
D = 64
INNER = 128
STATES = 16
HID = 128
EXPERTS = 16
LAYERS = 2
HALF = T // 2
TILES = T // P
GROUPS = 64
GROUPS_IMG = GROUPS // IMAGES
GROUP = T // GROUPS_IMG
STEPS = STATES
EPS = 1e-5

USE_Q, USE_S, USE_CONV, USE_GATE, USE_BC, USE_DT = 0, 2, 18, 20, 22, 24
WORK_USES = 26
SCORES = []
for _count in (0, 2, 2, 2, 1, 2, 2, 2, 1, 2, 0, 0, 0, 0, 0, 0):
    _first = sum(len(x) for x in SCORES)
    SCORES.append(range(_first, _first + _count))
USE_YT, USE_OUT1, USE_X1, USE_H1, USE_F0, USE_L1, USE_L2, USE_OUT2 = 0, 2, 3, 4, 5, 7, 9, 11
TAIL_USES = 12
TAIL_SETUP = 2
EARLY, LATE = 0, 1
TAIL_AT = {
    (2, LATE): USE_YT, (3, LATE): USE_YT + 1, (4, LATE): USE_OUT1, (5, LATE): USE_X1, (9, LATE): USE_H1,
    (10, LATE): USE_F0, (11, EARLY): USE_F0 + 1, (11, LATE): USE_L1, (12, EARLY): USE_L1 + 1,
    (12, LATE): USE_L2, (13, EARLY): USE_L2 + 1, (13, LATE): USE_OUT2,
}
LAST_STEPS = STEPS + 2

PACK = [
    ("wqb", P), ("wkb", P), ("wvb", P), ("wo_tok", D), ("w_main_t", 2 * D), ("w_conv", INNER), ("b_main", 1),
    ("b_conv", 1), ("bo_tok", 1), ("prelu_a", 1), ("a_log", STATES),
    ("ident", P), ("w_gate", INNER), ("b_gate", 1), ("w_bc", 4 * 2 * STATES), ("b_bc", 1),
    ("w_dt", INNER), ("b_dt", 1), ("w_out", D), ("b_out", 1), ("w_i", HID), ("b_i", 1),
    ("w_o", D), ("b_o", D), ("b_r", LAYERS * HID), ("b_s", LAYERS), ("w_s", LAYERS * HID), ("expert", 1),
]
PACK_AT = {}
PACK_COLS = 0
for _name, _cols in PACK:
    PACK_AT[_name] = (PACK_COLS, _cols)
    PACK_COLS += _cols
PACK_FIRST = PACK_AT["ident"][0]


def vit_layer(nc, xT, gammaT, packed, routed_w, route, out):
    with ExitStack() as ctx:
        def sb(name, shape, dt=F32):
            return ctx.enter_context(nc.sbuf_tensor(name, shape, dt))

        def ps(name, shape):
            return ctx.enter_context(nc.psum_tensor(name, shape, F32))

        def sem(name):
            return ctx.enter_context(nc.semaphore(name))

        pack = sb("pack", [P, PACK_COLS])
        gam = sb("gam", [P, TILES, T])
        expert_w = sb("expert_w", [P, LAYERS, EXPERTS + 1, HID])
        group_w = sb("group_w", [P, GROUPS_IMG, LAYERS, HID])
        sel = sb("sel", [P, STATES, P], BF16)
        wvo = sb("wvo", [P, D])
        wqk = sb("wqk", [P, P])
        w_mc = sb("w_mc", [P, INNER])
        b_mc = sb("b_mc", [P, 1])
        neg_a = sb("neg_a", [P, STATES])
        route_i = sb("route_i", [EXPERTS, GROUPS], I32)
        route_f = sb("route_f", [EXPERTS, GROUPS])
        onehot = sb("onehot", [EXPERTS, GROUPS])
        route_ok = sb("route_ok", [1, 2, GROUPS])
        route_x = sb("route_x", [1, GROUPS], I32)
        group_b = sb("group_b", [P, LAYERS, GROUPS])
        ln_s = sb("ln_s", [P, 5, TILES])

        x_in = sb("x_in", [P, T])
        qT = sb("qT", [P, T])
        sp_pos = sb("sp_pos", [P, T])
        v_sb = sb("v_sb", [P, TILES, D])
        mixed = sb("mixed", [P, 2, T])
        pre = sb("pre", [P, 2, HALF])
        hT = sb("hT", [P, 2, HALF])
        bc = mixed[:, 0, :]
        xc = mixed[:, 1, :]
        gate = sb("gate", [P, 2, T])
        bc3 = sb("bc3", [P, 2, T], BF16)
        delta = sb("delta", [P, 2, T])
        u = sb("u", [P, 2, T])
        decay = sb("decay", [P, 2, T])
        ub = sb("ub", [P, 2, T])
        h = sb("h", [P, 3, T])
        c_row = sb("c_row", [P, 4, T])
        hc = sb("hc", [P, 2, T])
        y_t = sb("y_t", [P, T])
        h1T = y_t[:, 0:HALF]
        ln_x = sb("ln_x", [P, HALF])
        ln_q = sb("ln_q", [P, HALF])
        h1 = sb("h1", [P, HALF])
        h1b = sb("h1b", [P, HALF])
        f = sb("f", [P, T])
        yg = f
        res = ln_q

        acc_y = ps("acc_y", [P, T])
        b_row = ps("b_row", [P, T])
        work = ps("work", [P, T])
        acc_r = ps("acc_r", [P, HALF])
        tail = ps("tail", [P, HALF])

        c_dram = nc.dram_tensor("c_dram", (IMAGES, STATES, T), F32, kind="Internal").ap()

        def const(name, rows=P, row0=0):
            at, cols = PACK_AT[name]
            return pack[row0:row0 + rows, at:at + cols]

        ident = const("ident")
        w_bc4 = const("w_bc")

        s_pack = sem("first_constants_loaded")
        s_pack2 = sem("constants_loaded")
        s_gam = [sem(f"gamma_loaded_{j}") for j in range(TILES)]
        s_x = sem("x_loaded")
        s_route = sem("route_loaded")
        s_rw = sem("expert_weights_loaded")
        s_ones = sem("ones_row_set")
        s_sel0 = sem("selector_zeroed")
        s_sel = sem("selector_ready")
        s_wvo = sem("folded_weights_ready")
        s_ea = sem("exp_a_ready")
        s_na = sem("neg_a_ready")
        s_rt = sem("route_steps")
        s_gb = sem("group_bias_ready")
        s_ws = sem("shared_weights_ready")
        s_cw = sem("combined_weights_ready")
        s_gw = [sem(f"group_weights_loaded_{g}") for g in range(2)]

        work_full = sem("work_full")
        work_read = sem("work_read")
        tail_full = sem("tail_full")
        tail_read = sem("tail_read")
        v_full = sem("v_full")
        v_ready = sem("v_ready")
        gv_done = sem("mixed_used")
        prelu_part = sem("prelu_parts")
        h_ready = sem("h_ready")
        bc_hi = sem("bc_high_ready")
        bc_rest = sem("bc_rest_ready")
        bc_mid = sem("bc_middle_ready")
        bc_rest2 = sem("bc_rest2_ready")
        bc_split = sem("bc_split_ready")
        c_stored = sem("c_stored")
        sp_step = sem("softplus_steps")
        delta_ready = sem("delta_ready")
        u_ready = sem("u_ready")

        b_ready = sem("b_row_ready")
        decay_ready = sem("decay_ready")
        ub_ready = sem("ub_ready")
        scan_done = sem("scan_done")
        c_loaded = [sem(f"c_row_loaded_{i}") for i in range(4)]
        hc_ready = sem("hc_ready")
        hc_used = sem("hc_used")
        y_read = sem("y_read")

        ln_sum = sem("ln_sum")
        ln_cent = sem("ln_centred")
        ln_sq = sem("ln_squared")
        ln_var = sem("ln_variance")
        ln_std = sem("ln_variance_eps")
        ln_log = sem("ln_log_steps")
        ln_pow = sem("ln_scale_ready")
        ln_out = sem("ln_out")
        h1b_ready = sem("h1_with_bias")
        stored = sem("out_stored")

        PHASES = range(-1, IMAGES + 2)

        def last_steps(p, n):
            return [(b, m) for b, m in ((p - 2, n + STEPS), (p - 1, n)) if 0 <= b < IMAGES and m < LAST_STEPS]

        def step_of(p, n):
            head = p + 1 if p + 1 < IMAGES else None
            scan = p if 0 <= p < IMAGES else None
            return head, scan, last_steps(p, n), STEPS * p + n

        def work_use(image, use):
            return WORK_USES * image + use

        def tail_use(image, use):
            return TAIL_SETUP + TAIL_USES * image + use

        def tail_to_read(n, half_step):
            return TAIL_AT.get((n, EARLY) if half_step == LATE else (n - 1, LATE))

        def bcast(ap, shape):
            return ap.unsqueeze(2).broadcast_to(shape)

        block = ctx.enter_context(nc.Block())

        @block.sync
        def _(sp):
            sp.dma_start(x_in[0:D, :], xT[0]).then_inc(s_x, 16)
            sp.dma_start(gam[:, 0, :], gammaT[0:P, :]).then_inc(s_gam[0], 16)
            for j in range(1, TILES):
                sp.dma_start(gam[:, j, :], gammaT[j * P:(j + 1) * P, :]).then_inc(s_gam[j], 16)
            sp.dma_start(expert_w[:, :, 0:EXPERTS, :], routed_w).then_inc(s_rw, 16)

            def load_c(k):
                b, n = k // STEPS, k % STEPS
                if n == 0:
                    sp.wait_ge(c_stored, 16 * (b + 1))
                if k >= 4:
                    sp.wait_ge(hc_ready, k - 3)
                sp.dma_start(c_row[:, k % 4, :], c_dram[b, n, :].partition_broadcast(P)).then_inc(c_loaded[k % 4], 16)

            def load_group(b, g):
                if b >= 1:
                    sp.wait_ge(tail_full, tail_use(b - 1, USE_L2 + g // 8) + 1)
                e = sp.value_load(route_x[0:1, GROUPS_IMG * b + g:GROUPS_IMG * b + g + 1],
                                  min_val=0, max_val=EXPERTS)
                sp.dma_start(group_w[:, g, :, :].unsqueeze(2), expert_w[:, :, bass.ds(e, 1), :])\
                    .then_inc(s_gw[g // 8], 16)

            for p in PHASES:
                for n in range(STEPS):
                    head, scan, last, k = step_of(p, n)
                    if head is not None and n == 11 and head + 1 < IMAGES:
                        sp.wait_ge(work_full, work_use(head, USE_CONV))
                        sp.dma_start(x_in[0:D, :], xT[head + 1]).then_inc(s_x, 16)
                    if head is not None and n == 14:
                        sp.wait_ge(work_read, work_use(head, USE_BC) + 2)
                        sp.dma_start(c_dram[head], mixed[STATES:2 * STATES, 0, :]).then_inc(c_stored, 16)
                    for ahead in {13: (), 14: (k + 2, k + 3)}.get(n, (k + 3,)):
                        if 0 <= ahead < STEPS * IMAGES:
                            load_c(ahead)
                    for b, m in last:
                        if m < 8:
                            if b == 0 and m == 0:
                                sp.wait_ge(s_rt, 5)
                                sp.wait_ge(s_cw, 3)
                            load_group(b, 2 * m)
                            load_group(b, 2 * m + 1)
                        if m == STEPS + 1:
                            sp.wait_ge(ln_out, 2 * b + 2)
                            for i in range(2):
                                sp.dma_start(out[b, i * HALF:(i + 1) * HALF, :].rearrange("(c t) d -> t c d", t=P),
                                             res[:, :].rearrange("p (c i d) -> p i c d", d=D, i=2)[:, i, :, :])\
                                    .then_inc(stored, 16)
            sp.wait_ge(stored, 32 * IMAGES)

        @block.tensor
        def _(pe):
            pe.wait_ge(s_pack, 16)
            nc.tensor.matmul(tail[:, 0:D], const("wvb", D), const("wo_tok", D), start=True, stop=True)
            nc.tensor.matmul(tail[:, D:D + P], const("wqb", D), const("wkb", D), start=True, stop=True)
            nc.tensor.matmul(tail[:, 192:192 + INNER], const("w_main_t"), const("w_conv"), start=True, stop=True)
            nc.tensor.matmul(tail[:, 320:321], const("w_conv"), const("b_main"), start=True, stop=True)\
                .then_inc(tail_full, 1)

            def begin_work(image, use):
                if work_use(image, use) >= 2:
                    pe.wait_ge(work_read, work_use(image, use) - 1)

            def begin_tail(image, use):
                pe.wait_ge(tail_read, tail_use(image, use))

            def project(image, use, weights, moving):
                for i in range(2):
                    begin_work(image, use + i)
                    nc.tensor.matmul(work[:, i * HALF:(i + 1) * HALF], weights, moving[:, i * HALF:(i + 1) * HALF],
                                     start=True, stop=True).then_inc(work_full, 1)

            def states_in(k):
                b, n = k // STEPS, k % STEPS
                if n == 0:
                    pe.wait_ge(bc_split, b + 1)
                    if b == 0:
                        pe.wait_ge(s_sel, 1)
                if k:
                    pe.wait_ge(ub_ready, k)
                for i in range(2):
                    mm = nc.tensor.matmul(b_row[:, i * HALF:(i + 1) * HALF], sel[:, n, :],
                                          bc3[:, b % 2, i * HALF:(i + 1) * HALF], start=True, stop=True)
                mm.then_inc(b_ready, 1)

            def states_out(k):
                b, n = k // STEPS, k % STEPS
                pe.wait_ge(hc_ready, k + 1)
                if n == 0 and b:
                    pe.wait_ge(y_read, b)
                for c in range(TILES):
                    mm = nc.tensor.matmul(acc_y[:, c * P:(c + 1) * P], hc[:, k % 2, c * P:(c + 1) * P], ident,
                                          start=(n == 0 and c % 4 == 0), stop=(n == STATES - 1), is_transpose=True,
                                          skip_group_check=True)
                mm.then_inc(hc_used, 1)

            def head_part(b, n):
                if n == 0:
                    pe.wait_ge(s_x, 16 * (b + 1))
                    if b == 0:
                        pe.wait_ge(s_ones, 2)
                        pe.wait_ge(s_wvo, 4)
                    project(b, USE_Q, wqk[:, :], x_in)
                    if b:
                        pe.wait_ge(prelu_part, 2 * b)
                    for c in range(TILES):
                        mm = nc.tensor.matmul(acc_r[:, c * D:(c + 1) * D], x_in[:, c * P:(c + 1) * P],
                                              wvo[:, :], start=True, stop=True)
                    mm.then_inc(v_full, 1)
                for unit in SCORES[n - 1] if n else ():
                    j = unit // 2
                    if unit % 2 == 0:
                        continue
                    pe.wait_ge(work_read, work_use(b, USE_S + unit) + 1)
                    if j == 0:
                        pe.wait_ge(v_ready, b + 1)
                    for i in range(2):
                        mm = nc.tensor.matmul(acc_r[D * i:D * i + D, :], v_sb[:, j, :],
                                              mixed[:, j % 2, i * HALF:(i + 1) * HALF],
                                              start=(j == 0), stop=(j == TILES - 1), skip_group_check=True)
                    mm.then_inc(gv_done, 1)
                for unit in SCORES[n + 1] if n + 1 < STEPS else ():
                    j, i = unit // 2, unit % 2
                    begin_work(b, USE_S + unit)
                    if unit == 0:
                        pe.wait_ge(work_read, work_use(b, USE_S))
                    nc.tensor.matmul(work[:, i * HALF:(i + 1) * HALF], x_in[:, j * P:(j + 1) * P],
                                     qT[:, i * HALF:(i + 1) * HALF], start=True, stop=True).then_inc(work_full, 1)
                if n in (11, 12):
                    head_projections(b, n, LATE)

            def head_projections(b, n, half_step):
                if n == 11:
                    if half_step == EARLY:
                        pe.wait_ge(h_ready, b + 1)
                        if b == 0:
                            pe.wait_ge(s_pack2, 16)
                    use, weights = ((USE_CONV, w_mc), (USE_GATE, const("w_gate")))[half_step]
                    for i in range(2):
                        begin_work(b, use + i)
                        nc.tensor.matmul(work[:, i * HALF:(i + 1) * HALF], weights[D * i:D * i + D, :],
                                         hT[D * i:D * i + D, b % 2, :], start=True, stop=True).then_inc(work_full, 1)
                if n == 12:
                    if half_step == EARLY:
                        pe.wait_ge(work_read, work_use(b, USE_CONV) + 2)
                        project(b, USE_BC, const("w_bc"), xc)
                    else:
                        project(b, USE_DT, const("w_dt"), xc)

            def last_part(b, n, half_step):
                use = TAIL_AT.get((n, half_step))
                if use is None:
                    return
                begin_tail(b, use)
                if use in (USE_YT, USE_YT + 1):
                    i = use - USE_YT
                    pe.wait_ge(y_read, b + 1)
                    for c in range(4 * i, 4 * i + 4):
                        mm = nc.tensor.transpose(tail[:, (c % 4) * P:(c % 4 + 1) * P], y_t[:, c * P:(c + 1) * P], ident)
                elif use == USE_OUT1:
                    pe.wait_ge(tail_read, tail_use(b, USE_YT) + 2)
                    for i in range(2):
                        mm = nc.tensor.matmul(tail[D * i:D * i + D, :], const("w_out"), yg[:, i * HALF:(i + 1) * HALF],
                                              start=True, stop=True, skip_group_check=True)
                elif use == USE_X1:
                    pe.wait_ge(tail_read, tail_use(b, USE_OUT1) + 1)
                    for c in range(TILES // 2):
                        mm = nc.tensor.transpose(tail[:, c * P:(c + 1) * P], yg[:, c * P:(c + 1) * P], ident)
                elif use == USE_H1:
                    pe.wait_ge(ln_out, 2 * b + 1)
                    for c in range(TILES // 2):
                        mm = nc.tensor.transpose(tail[:, c * P:(c + 1) * P], h1[:, c * P:(c + 1) * P], ident)
                elif use in (USE_F0, USE_F0 + 1):
                    i = use - USE_F0
                    mm = nc.tensor.matmul(tail[:, :], const("w_i", D, D * i), h1T[D * i:D * i + D, :],
                                          start=True, stop=True)
                elif use in (USE_L1, USE_L1 + 1, USE_L2, USE_L2 + 1):
                    layer, i = (use - USE_L1) // 2, (use - USE_L1) % 2
                    if layer == 0:
                        pe.wait_ge(s_gw[i], 16 * 8 * (b + 1))
                    for g in range(8 * i, 8 * i + 8):
                        mm = nc.tensor.matmul(tail[:, (g % 8) * GROUP:(g % 8 + 1) * GROUP], group_w[:, g, layer, :],
                                              f[:, g * GROUP:(g + 1) * GROUP], start=True, stop=True)
                elif use == USE_OUT2:
                    for c in range(TILES):
                        at = (2 * (c % 4) + c // 4) * D
                        mm = nc.tensor.matmul(tail[:, at:at + D], f[:, c * P:(c + 1) * P], const("w_o"),
                                              start=True, stop=True)
                mm.then_inc(tail_full, 1)

            for p in PHASES:
                for n in range(STEPS):
                    head, scan, last, k = step_of(p, n)
                    if 0 <= k + 1 < STEPS * IMAGES:
                        states_in(k + 1)
                    for b, m in last:
                        last_part(b, m, EARLY)
                    if head is not None:
                        head_projections(head, n, EARLY)
                    if 0 <= k - 2 < STEPS * IMAGES:
                        states_out(k - 2)
                    if head is not None:
                        head_part(head, n)
                    for b, m in last:
                        last_part(b, m, LATE)
                    if p == -1 and n == 13:
                        pe.wait_ge(s_rt, 2)
                        pe.wait_ge(tail_read, 1)
                        for layer in range(LAYERS):
                            mm = nc.tensor.matmul(tail[:, layer * GROUPS:(layer + 1) * GROUPS],
                                                  const("b_r", EXPERTS)[:, layer * HID:(layer + 1) * HID],
                                                  onehot[:, :], start=True, stop=True)
                        mm.then_inc(tail_full, 1)

        @block.scalar
        def _(act):
            act.dma_start(pack[:, 0:PACK_FIRST], packed[:, 0:PACK_FIRST]).then_inc(s_pack, 16)
            act.dma_start(pack[:, PACK_FIRST:], packed[:, PACK_FIRST:]).then_inc(s_pack2, 16)
            act.preload_act_table_set("natural_log_exp_and_others")
            act.dma_start(route_i[:, :], route.partition_broadcast(EXPERTS)).then_inc(s_route, 16)
            act.wait_ge(s_pack, 16)
            nc.scalar.activation(neg_a[:, :], const("a_log"), ACT.Exp).then_inc(s_ea, 1)

            def decay_of(k):
                b, n = k // STEPS, k % STEPS
                if n == 0:
                    act.wait_ge(delta_ready, b + 1)
                    if b == 0:
                        act.wait_ge(s_na, 1)
                if k >= 2:
                    act.wait_ge(scan_done, k - 1)
                nc.scalar.activation(decay[:, k % 2, :], delta[:, b % 2, :], ACT.Exp, scale=neg_a[:, n:n + 1])\
                    .then_inc(decay_ready, 1)

            def halves(b, use, dst, func, **kw):
                for i in range(2):
                    act.wait_ge(work_full, work_use(b, use + i) + 1)
                    nc.scalar.activation(dst[:, i * HALF:(i + 1) * HALF], work[:, i * HALF:(i + 1) * HALF], func, **kw)\
                        .then_inc(work_read, 1)

            def gates(b):
                if b >= 2:
                    act.wait_ge(tail_read, tail_use(b - 2, USE_YT + 1) + 1)
                halves(b, USE_GATE, gate[:, b % 2, :], ACT.Silu, bias=const("b_gate"))
                act.preload_act_table_set("natural_log_exp_and_others")

            def head_part(b, n):
                if n == 0:
                    if b:
                        act.wait_ge(bc_split, b)
                    halves(b, USE_Q, qT, ACT.Copy)
                    act.wait_ge(v_full, b + 1)
                    nc.scalar.activation(v_sb[:, :, :], acc_r[:, :].rearrange("p (c d) -> p c d", d=D), ACT.Copy)\
                        .then_inc(v_ready, 1)
                if n == 11:
                    if b == 0:
                        act.wait_ge(s_wvo, 4)
                        act.wait_ge(s_pack2, 16)
                    halves(b, USE_CONV, xc, ACT.Silu, bias=b_mc[:, :])
                if n == 12:
                    halves(b, USE_BC, bc, ACT.Identity, bias=const("b_bc"))
                    act.wait_ge(work_read, work_use(b, USE_BC) + 2)
                    if b >= 2:
                        act.wait_ge(b_ready, STEPS * (b - 1))
                    nc.scalar.activation(bc3[:, b % 2, :], bc, ACT.Copy).then_inc(bc_hi, 1)
                if n == 13:
                    if b >= 2:
                        act.wait_ge(decay_ready, STEPS * (b - 1))
                    if b:
                        act.wait_ge(delta_ready, b)
                    for i in range(2):
                        act.wait_ge(work_full, work_use(b, USE_DT + i) + 1)
                        at = slice(i * HALF, (i + 1) * HALF)
                        nc.scalar.activation(delta[:, b % 2, at], work[:, at], ACT.Abs, bias=const("b_dt"))\
                            .then_inc(sp_step, 1)
                        nc.scalar.activation(sp_pos[:, at], work[:, at], ACT.Relu, bias=const("b_dt"))\
                            .then_inc(work_read, 1)
                    act.wait_ge(sp_step, 4 * b + 2)
                    nc.scalar.activation(delta[:, b % 2, :], delta[:, b % 2, :], ACT.Exp, scale=-1.0).then_inc(sp_step, 1)
                    act.wait_ge(sp_step, 4 * b + 3)
                    nc.scalar.activation(delta[:, b % 2, :], delta[:, b % 2, :], ACT.Ln, bias=1.0).then_inc(sp_step, 1)
                    act.wait_ge(bc_rest, b + 1)
                    nc.scalar.activation(bc3[D:P, b % 2, :], qT[D:P, :], ACT.Copy).then_inc(bc_mid, 1)
                if n == 14:
                    act.wait_ge(bc_rest2, b + 1)
                    nc.scalar.activation(bc3[96:P, b % 2, :], qT[96:P, :], ACT.Copy).then_inc(bc_split, 1)

            def last_part(b, n, half_step):
                if (n, half_step) == (1, LATE):
                    act.wait_ge(hc_used, STEPS * (b + 1))
                    nc.scalar.activation(y_t[:, :], acc_y[:, :], ACT.Copy).then_inc(y_read, 1)
                if (n, half_step) in ((8, EARLY), (STEPS, EARLY)):
                    count = 2 * b + (n == STEPS)
                    act.wait_ge(ln_std, count + 1)
                    nc.scalar.activation(ln_s[:, 3, :], ln_s[:, 2, :], ACT.Ln).then_inc(ln_log, 1)
                    act.wait_ge(ln_log, 2 * count + 1)
                    nc.scalar.activation(ln_s[:, 3, :], ln_s[:, 3, :], ACT.Exp, scale=-0.5).then_inc(ln_log, 1)
                use = tail_to_read(n, half_step)
                if use == USE_H1:
                    act.wait_ge(tail_full, tail_use(b, use) + 1)
                    nc.scalar.activation(h1T, tail[:, :], ACT.Copy).then_inc(tail_read, 1)
                if use in (USE_F0, USE_F0 + 1):
                    i = use - USE_F0
                    act.wait_ge(tail_full, tail_use(b, use) + 1)
                    nc.scalar.activation(f[:, i * HALF:(i + 1) * HALF], tail[:, :], ACT.Relu, bias=const("b_i"))\
                        .then_inc(tail_read, 1)
                if use in (USE_L1, USE_L1 + 1, USE_L2, USE_L2 + 1):
                    layer, i = (use - USE_L1) // 2, (use - USE_L1) % 2
                    act.wait_ge(tail_full, tail_use(b, use) + 1)
                    for g in range(8 * i, 8 * i + 8):
                        op = nc.scalar.activation(f[:, g * GROUP:(g + 1) * GROUP],
                                                  tail[:, (g % 8) * GROUP:(g % 8 + 1) * GROUP], ACT.Relu,
                                                  bias=group_b[:, layer, GROUPS_IMG * b + g:GROUPS_IMG * b + g + 1])
                    op.then_inc(tail_read, 1)

            for p in PHASES:
                for n in range(STEPS):
                    head, scan, last, k = step_of(p, n)
                    for b, m in last:
                        last_part(b, m, EARLY)
                    if head is not None and n == 12:
                        gates(head)
                    if 0 <= k + 1 < STEPS * IMAGES:
                        decay_of(k + 1)
                    if head is not None:
                        head_part(head, n)
                    for b, m in last:
                        last_part(b, m, LATE)

        @block.gpsimd
        def _(pool):
            nc.gpsimd.memset(sel[:, :, :], 0.0).then_inc(s_sel0, 1)
            for i, lo in enumerate((0, 64, 96)):
                pool.wait_ge(s_sel0, i + 1)
                nc.gpsimd.affine_select(out=sel[:, :, :], in_=sel[:, :, :], compare_op=ALU.not_equal, fill=1.0,
                                        base=-lo, pattern=[[-1, STATES], [0, P]], channel_multiplier=1)\
                    .then_inc(s_sel if lo == 96 else s_sel0, 1)

            def combine_weights():
                pool.wait_ge(s_pack2, 16)
                for layer in range(LAYERS):
                    at = PACK_AT["w_s"][0] + layer * HID
                    nc.gpsimd.tensor_tensor(expert_w[:, layer, EXPERTS, :], pack[:, at:at + HID], ident, ALU.add)\
                        .then_inc(s_ws, 1)
                pool.wait_ge(s_ws, 2)
                pool.wait_ge(s_rw, 16)
                for layer in range(LAYERS):
                    w = expert_w[:, layer, 0:EXPERTS, :]
                    nc.gpsimd.tensor_tensor(w, w, expert_w[:, layer, EXPERTS, :].unsqueeze(1)
                                            .broadcast_to([P, EXPERTS, HID]), ALU.add).then_inc(s_cw, 1)
                pool.wait_ge(s_cw, 2)
                pool.sem_inc(s_cw, 1)

            def weigh(k):
                pool.wait_ge(scan_done, k + 1)
                pool.wait_ge(c_loaded[k % 4], 16 * (k // 4 + 1))
                if k >= 2:
                    pool.wait_ge(hc_used, k - 1)
                nc.gpsimd.tensor_tensor(hc[:, k % 2, :], h[:, k % 3, :], c_row[:, k % 4, :], ALU.mult)\
                    .then_inc(hc_ready, 1)

            def head_part(b, n):
                if n == 12:
                    pool.wait_ge(bc_hi, b + 1)
                    nc.gpsimd.tensor_tensor(qT[:, :], bc, bc3[:, b % 2, :], ALU.subtract).then_inc(bc_rest, 1)
                if n == 13:
                    pool.wait_ge(sp_step, 4 * b + 4)
                    pool.wait_ge(work_read, work_use(b, USE_DT) + 2)
                    nc.gpsimd.tensor_tensor(delta[:, b % 2, :], delta[:, b % 2, :], sp_pos[:, :], ALU.add)\
                        .then_inc(delta_ready, 1)
                if n == 14:
                    pool.wait_ge(delta_ready, b + 1)
                    if b >= 2:
                        pool.wait_ge(ub_ready, STEPS * (b - 1))
                    nc.gpsimd.tensor_tensor(u[:, b % 2, :], delta[:, b % 2, :], xc, ALU.mult).then_inc(u_ready, 1)

            def last_part(b, n):
                if n == 6:
                    pool.wait_ge(tail_read, tail_use(b, USE_X1) + 1)
                    if b:
                        pool.wait_ge(stored, 32 * b)
                    nc.gpsimd.tensor_tensor(ln_q[:, :], ln_x[:, :], ln_x[:, :], ALU.mult).then_inc(ln_sq, 1)
                if n == 10:
                    pool.wait_ge(ln_out, 2 * b + 1)
                    if b:
                        pool.wait_ge(tail_read, tail_use(b - 1, USE_OUT2) + 1)
                    nc.gpsimd.tensor_tensor(h1b[:, :].rearrange("p (c d) -> p c d", d=D),
                                            h1[:, :].rearrange("p (c d) -> p c d", d=D),
                                            const("b_o").unsqueeze(1).broadcast_to([P, TILES, D]), ALU.add)\
                        .then_inc(h1b_ready, 1)
                if n == 14:
                    pool.wait_ge(ln_cent, b + 1)
                    if b:
                        pool.wait_ge(stored, 32 * b)
                    nc.gpsimd.tensor_tensor(ln_q[:, :], ln_x[:, :], ln_x[:, :], ALU.mult).then_inc(ln_sq, 1)
                if n in (8, STEPS):
                    count = 2 * b + (n == STEPS)
                    v, r, t = ln_s[:, 2, :], ln_s[:, 3, :], ln_s[:, 4, :]
                    pool.wait_ge(ln_log, 2 * count + 2)
                    nc.gpsimd.tensor_tensor(t, r, r, ALU.mult).then_inc(ln_pow, 1)
                    pool.wait_ge(ln_pow, 4 * count + 1)
                    nc.gpsimd.tensor_tensor(t, t, v, ALU.mult).then_inc(ln_pow, 1)
                    pool.wait_ge(ln_pow, 4 * count + 2)
                    nc.gpsimd.tensor_scalar(t, t, -0.5, 1.5, ALU.mult, ALU.add).then_inc(ln_pow, 1)
                    pool.wait_ge(ln_pow, 4 * count + 3)
                    nc.gpsimd.tensor_tensor(r, r, t, ALU.mult).then_inc(ln_pow, 1)

            for p in PHASES:
                for n in range(STEPS):
                    head, scan, last, k = step_of(p, n)
                    if 0 <= k - 1 < STEPS * IMAGES:
                        weigh(k - 1)
                    if head is not None:
                        head_part(head, n)
                    for b, m in last:
                        last_part(b, m)
                    if p == -1 and n == 10:
                        combine_weights()

        @block.vector
        def _(dve):
            nc.vector.memset(x_in[D:P, :], 0.0).then_inc(s_ones, 1)
            dve.wait_ge(s_ones, 1)
            nc.vector.memset(x_in[D:D + 1, :], 1.0).then_inc(s_ones, 1)
            dve.wait_ge(tail_full, 1)
            dve.wait_ge(s_pack, 16)
            nc.vector.tensor_copy(wqk[:, :], tail[:, D:D + P]).then_inc(s_wvo, 1)
            nc.vector.tensor_copy(wvo[:, :], tail[:, 0:D]).then_inc(s_wvo, 1)
            nc.vector.tensor_copy(w_mc[:, :], tail[:, 192:192 + INNER]).then_inc(s_wvo, 1)
            nc.vector.tensor_tensor(b_mc[:, :], tail[:, 320:321], const("b_conv"), ALU.add).then_inc(s_wvo, 1)
            dve.wait_ge(s_wvo, 4)
            dve.sem_inc(tail_read, 1)
            dve.wait_ge(s_ea, 1)
            nc.vector.tensor_scalar(neg_a[:, :], neg_a[:, :], -1.0, None, ALU.mult).then_inc(s_na, 1)

            def routes():
                dve.wait_ge(s_route, 16)
                dve.wait_ge(s_pack2, 16)
                nc.vector.tensor_copy(route_f[:, :], route_i[:, :]).then_inc(s_rt, 1)
                dve.wait_ge(s_rt, 1)
                nc.vector.tensor_scalar(onehot[:, :], route_f[:, :], const("expert", EXPERTS), None, ALU.is_equal)\
                    .then_inc(s_rt, 1)
                nc.vector.tensor_scalar(route_ok[:, 0, :], route_f[0:1, :], 0.0, None, ALU.is_ge).then_inc(s_rt, 1)
                dve.wait_ge(s_rt, 3)
                nc.vector.scalar_tensor_tensor(out=route_ok[:, 1, :], in0=route_f[0:1, :], scalar=float(EXPERTS - 1),
                                               in1=route_ok[:, 0, :], op0=ALU.is_le, op1=ALU.mult).then_inc(s_rt, 1)
                dve.wait_ge(s_rt, 4)
                nc.vector.scalar_tensor_tensor(out=route_ok[:, 0, :], in0=route_f[0:1, :], scalar=float(EXPERTS),
                                               in1=route_ok[:, 1, :], op0=ALU.subtract, op1=ALU.mult)\
                    .then_inc(s_gb, 1)
                dve.wait_ge(s_gb, 1)
                nc.vector.tensor_scalar(route_x[:, :], route_ok[:, 0, :], float(EXPERTS), None, ALU.add)\
                    .then_inc(s_rt, 1)

            def group_bias():
                dve.wait_ge(tail_full, 2)
                for layer in range(LAYERS):
                    at = PACK_AT["b_s"][0] + layer
                    op = nc.vector.tensor_scalar(group_b[:, layer, :], tail[:, layer * GROUPS:(layer + 1) * GROUPS],
                                                 pack[:, at:at + 1], None, ALU.add)
                op.then_inc(tail_read, 1)

            def drive(k):
                b, n = k // STEPS, k % STEPS
                if n == 0:
                    dve.wait_ge(u_ready, b + 1)
                dve.wait_ge(b_ready, k + 1)
                if k >= 2:
                    dve.wait_ge(scan_done, k - 1)
                nc.vector.tensor_tensor(ub[:, k % 2, :], u[:, b % 2, :], b_row[:, :], ALU.mult).then_inc(ub_ready, 1)

            def scan_step(k):
                dve.wait_ge(ub_ready, k + 1)
                dve.wait_ge(decay_ready, k + 1)
                if k >= 3:
                    dve.wait_ge(hc_ready, k - 2)
                nc.vector.tensor_tensor_scan(h[:, k % 3, :], decay[:, k % 2, :], ub[:, k % 2, :], 0.0,
                                             ALU.mult, ALU.add).then_inc(scan_done, 1)

            def head_part(b, n):
                for unit in SCORES[n]:
                    j, i = unit // 2, unit % 2
                    at = slice(i * HALF, (i + 1) * HALF)
                    if b == 0:
                        dve.wait_ge(s_gam[j], 16)
                    dve.wait_ge(work_full, work_use(b, USE_S + unit) + 1)
                    if b and unit == 0:
                        dve.wait_ge(bc_rest, b)
                        dve.wait_ge(c_stored, 16 * b)
                    if b and unit == 2:
                        dve.wait_ge(u_ready, b)
                    if TILES * b + j >= 2 and i == 0:
                        dve.wait_ge(gv_done, TILES * b + j - 1)
                    nc.vector.tensor_tensor(mixed[:, j % 2, at], gam[:, j, at], work[:, at], ALU.mult)\
                        .then_inc(work_read, 1)
            def prelu(b):
                dve.wait_ge(gv_done, TILES * (b + 1))
                for i, op in enumerate((ALU.min, ALU.max)):
                    nc.vector.tensor_scalar(pre[:, i, :], acc_r[:, :], const("bo_tok"), 0.0, ALU.add, op)\
                        .then_inc(prelu_part, 1)
                dve.wait_ge(prelu_part, 2 * b + 2)
                if b >= 2:
                    dve.wait_ge(tail_read, tail_use(b - 2, USE_OUT1) + 1)
                nc.vector.scalar_tensor_tensor(out=hT[:, b % 2, :], in0=pre[:, 0, :], scalar=const("prelu_a"),
                                               in1=pre[:, 1, :], op0=ALU.mult, op1=ALU.add).then_inc(h_ready, 1)

            def rows(ap):
                return ap.rearrange("p (c d) -> p c d", d=D)

            def norm(count, part, dst, src=None):
                x3 = rows(ln_x[:, :])
                if part == 0:
                    nc.vector.tensor_reduce(ln_s[:, 0, :], src, AX.X, ALU.add).then_inc(ln_sum, 1)
                    dve.wait_ge(ln_sum, count + 1)
                    nc.vector.scalar_tensor_tensor(out=x3, in0=bcast(ln_s[:, 0, :], [P, TILES, D]), scalar=-1.0 / D,
                                                   in1=src, op0=ALU.mult, op1=ALU.add)\
                        .then_inc(tail_read if count % 2 == 0 else ln_cent, 1)
                if part == 1:
                    dve.wait_ge(ln_sq, count + 1)
                    nc.vector.tensor_reduce(ln_s[:, 1, :], rows(ln_q[:, :]), AX.X, ALU.add).then_inc(ln_var, 1)
                    dve.wait_ge(ln_var, count + 1)
                    nc.vector.tensor_scalar(ln_s[:, 2, :], ln_s[:, 1, :], 1.0 / D, EPS, ALU.mult, ALU.add)\
                        .then_inc(ln_std, 1)
                if part == 2:
                    dve.wait_ge(ln_pow, 4 * (count + 1))
                    nc.vector.tensor_tensor(dst, x3, bcast(ln_s[:, 3, :], [P, TILES, D]), ALU.mult).then_inc(ln_out, 1)

            def last_part(b, n, half_step):
                use = tail_to_read(n, half_step)
                if use in (USE_YT, USE_YT + 1):
                    at = slice((use - USE_YT) * HALF, (use - USE_YT + 1) * HALF)
                    dve.wait_ge(tail_full, tail_use(b, use) + 1)
                    dve.wait_ge(work_read, work_use(b, USE_GATE) + 2)
                    nc.vector.tensor_tensor(yg[:, at], gate[:, b % 2, at], tail[:, :], ALU.mult).then_inc(tail_read, 1)
                if use == USE_OUT1:
                    dve.wait_ge(tail_full, tail_use(b, use) + 1)
                    nc.vector.scalar_tensor_tensor(out=yg[:, 0:HALF], in0=tail[:, :], scalar=const("b_out"),
                                                   in1=hT[:, b % 2, :], op0=ALU.add, op1=ALU.add).then_inc(tail_read, 1)
                if use == USE_X1:
                    dve.wait_ge(tail_full, tail_use(b, use) + 1)
                    norm(2 * b, 0, None, rows(tail[:, :]))
                if use == USE_OUT2:
                    dve.wait_ge(tail_full, tail_use(b, use) + 1)
                    dve.wait_ge(h1b_ready, b + 1)
                    nc.vector.tensor_tensor(ln_x[:, :], tail[:, :], h1b[:, :], ALU.add).then_inc(tail_read, 1)
                    dve.wait_ge(tail_read, tail_use(b, use) + 1)
                    norm(2 * b + 1, 0, None, rows(ln_x[:, :]))
                if (n, half_step) == (7, LATE):
                    norm(2 * b, 1, None)
                if (n, half_step) == (9, EARLY):
                    if b:
                        dve.wait_ge(h1b_ready, b)
                    norm(2 * b, 2, rows(h1[:, :]))
                if (n, half_step) == (15, LATE):
                    norm(2 * b + 1, 1, None)
                if (n, half_step) == (STEPS + 1, EARLY):
                    norm(2 * b + 1, 2, rows(res[:, :]))

            for p in PHASES:
                for n in range(STEPS):
                    head, scan, last, k = step_of(p, n)
                    if scan is not None:
                        drive(k)
                    for b, m in last:
                        last_part(b, m, EARLY)
                    if head is not None:
                        head_part(head, n)
                    if scan is not None:
                        scan_step(k)
                    for b, m in last:
                        last_part(b, m, LATE)
                    if head is not None and n == 10:
                        prelu(head)
                    if head is not None and n == 13:
                        dve.wait_ge(bc_mid, head + 1)
                        nc.vector.tensor_tensor(qT[96:P, :], qT[96:P, :], bc3[96:P, head % 2, :], ALU.subtract)\
                            .then_inc(bc_rest2, 1)
                    if p == -1 and n == 1:
                        routes()
                    if p == -1 and n == 13:
                        group_bias()


def kernel(**inputs):
    import numpy as np
    import concourse.bacc as bacc
    from concourse.bass_utils import run_bass_kernel_spmd

    a = {name: np.ascontiguousarray(value) for name, value in inputs.items()}
    tok = {n[len("L0_tok_"):]: v for n, v in a.items() if n.startswith("L0_tok_")}
    att = {n[len("L0_attn_"):]: v for n, v in a.items() if n.startswith("L0_attn_")}
    ffn = {n[len("L0_ffn_"):]: v for n, v in a.items() if n.startswith("L0_ffn_")}

    packed = np.zeros((P, PACK_COLS), np.float32)

    def place(name, value, row0=0, col0=0):
        at = PACK_AT[name][0] + col0
        packed[row0:row0 + value.shape[0], at:at + value.shape[1]] = value

    for name, w, b in (("wqb", tok["Wq"], tok["bq"]), ("wkb", tok["Wk"], tok["bk"]), ("wvb", tok["Wv"], tok["bv"])):
        place(name, w.T)
        place(name, b[:, None], 0, D)
    for i in range(2):
        place("w_main_t", att["W_in"][:, 0:INNER].T, 0, D * i)
        place("w_gate", att["W_in"][:, INNER:], D * i)
        place("bo_tok", tok["bo"][:, None], D * i)
    place("b_main", att["b_in"][0:INNER, None])
    place("b_gate", att["b_in"][INNER:, None])
    place("wo_tok", tok["Wo"])
    place("prelu_a", np.broadcast_to(tok["prelu_a"].reshape(1, 1), (P, 1)))
    place("ident", np.eye(P, dtype=np.float32))
    place("w_conv", att["W_conv"])
    place("b_conv", att["b_conv"][:, None])
    for i in range(4):
        place("w_bc", att["W_bc"], 0, 2 * STATES * i)
        place("b_bc", att["b_bc"][:, None], 2 * STATES * i)
    place("w_dt", att["W_dt"])
    place("b_dt", att["b_dt"][:, None])
    place("a_log", att["A_log"])
    place("w_out", att["W_out"])
    for i in range(2):
        place("b_out", att["b_out"][:, None], D * i)
        place("w_i", ffn["Wi"].T, D * i)
    place("b_i", ffn["bi"][:, None])
    place("w_o", ffn["Wo"].T)
    place("b_o", np.broadcast_to(ffn["bo"], (P, D)))
    for layer in range(LAYERS):
        place("b_r", ffn["br"][layer], 0, HID * layer)
        place("b_s", ffn["bs"][layer, 0][:, None], 0, layer)
        place("w_s", ffn["Ws"][layer, 0].T, 0, HID * layer)
    place("expert", np.arange(EXPERTS, dtype=np.float32)[:, None])

    arrays = {
        "xT": np.ascontiguousarray(a["x"].reshape(IMAGES, T, D).transpose(0, 2, 1)),
        "gammaT": np.ascontiguousarray(tok["d_gamma_batched"].T),
        "packed": packed,
        "routed_w": np.ascontiguousarray(ffn["Wr"].transpose(3, 0, 1, 2)),
        "route": ffn["route_id"],
    }
    nc = bacc.Bacc("TRN2", target_bir_lowering=False, num_devices=1)
    args = [nc.dram_tensor(name, v.shape, mybir.dt.from_np(v.dtype), kind="ExternalInput").ap()
            for name, v in arrays.items()]
    out = nc.dram_tensor("out", (IMAGES, T, D), F32, kind="ExternalOutput").ap()
    vit_layer(nc, *args, out)
    result = run_bass_kernel_spmd(nc, [arrays], core_ids=[0])
    return result.results[0]["out"]
```

```python
from contextlib import ExitStack

import concourse.bass as bass
from concourse import mybir

F32 = mybir.dt.float32
BF16 = mybir.dt.bfloat16
I32 = mybir.dt.int32
ALU = mybir.AluOpType
ACT = mybir.ActivationFunctionType
AX = mybir.AxisListType

P = 128
IMAGES = 4
T = 1024
D = 64
INNER = 128
STATES = 16
HID = 128
EXPERTS = 16
LAYERS = 2
HALF = T // 2
TILES = T // P
GROUPS = 64
GROUPS_IMG = GROUPS // IMAGES
GROUP = T // GROUPS_IMG
STEPS = STATES
EPS = 1e-5

USE_Q, USE_S, USE_CONV, USE_GATE, USE_BC, USE_DT = 0, 2, 18, 20, 22, 24
WORK_USES = 26
SCORES = []
for _count in (0, 2, 2, 2, 2, 2, 2, 2, 2, 0, 0, 0, 0, 0, 0, 0):
    _first = sum(len(x) for x in SCORES)
    SCORES.append(range(_first, _first + _count))
USE_YT, USE_OUT1, USE_X1, USE_H1, USE_F0, USE_L1, USE_L2, USE_OUT2 = 0, 2, 3, 4, 5, 7, 9, 11
TAIL_USES = 12
TAIL_SETUP = 2
EARLY, LATE = 0, 1
TAIL_AT = {
    (2, LATE): USE_YT, (3, LATE): USE_YT + 1, (4, LATE): USE_OUT1, (5, LATE): USE_X1, (9, LATE): USE_H1,
    (11, LATE): USE_F0, (12, LATE): USE_F0 + 1, (13, LATE): USE_L1, (14, LATE): USE_L1 + 1,
    (15, LATE): USE_L2, (16, LATE): USE_L2 + 1, (17, LATE): USE_OUT2,
}
TAIL_FROM = {
    USE_OUT1: (USE_YT, USE_YT + 1), USE_X1: (USE_OUT1,), USE_F0: (USE_H1,), USE_F0 + 1: (USE_H1,),
    USE_L1: (USE_F0,), USE_L1 + 1: (USE_F0 + 1,), USE_L2: (USE_L1,), USE_L2 + 1: (USE_L1 + 1,),
    USE_OUT2: (USE_L2,),
}
LN_AT = (6, 18)
ALONE = IMAGES - 2
TAIL_AT_ALONE = {
    (2, LATE): USE_YT, (3, LATE): USE_YT + 1, (4, LATE): USE_OUT1, (5, LATE): USE_X1, (9, LATE): USE_H1,
    (10, LATE): USE_F0, (11, EARLY): USE_F0 + 1, (11, LATE): USE_L1, (12, LATE): USE_L1 + 1,
    (13, LATE): USE_L2, (14, LATE): USE_L2 + 1, (15, LATE): USE_OUT2,
}
LN_AT_ALONE = (6, 16)
LAST_STEPS = LN_AT[1] + 4

PACK = [
    ("wqb", P), ("wkb", P), ("wvb", P), ("wo_tok", D), ("w_main_t", 2 * D), ("w_conv", INNER), ("b_main", 1),
    ("b_conv", 1), ("bo_tok", 1), ("prelu_a", 1), ("a_log", STATES),
    ("ident", P), ("w_gate", 2 * INNER), ("b_gate", 1), ("w_bc", 4 * 2 * STATES), ("b_bc", 1),
    ("w_dt", INNER), ("b_dt", 1), ("w_out", D), ("b_out", 1), ("w_i", HID), ("b_i", 1),
    ("w_o", D), ("b_o", D), ("b_r", LAYERS * HID), ("b_s", LAYERS), ("w_s", LAYERS * HID), ("expert", 1),
]
PACK_AT = {}
PACK_COLS = 0
for _name, _cols in PACK:
    PACK_AT[_name] = (PACK_COLS, _cols)
    PACK_COLS += _cols
PACK_FIRST = PACK_AT["ident"][0]


def vit_layer(nc, xT, gammaT, packed, routed_w, route, out):
    with ExitStack() as ctx:
        def sb(name, shape, dt=F32):
            return ctx.enter_context(nc.sbuf_tensor(name, shape, dt))

        def ps(name, shape):
            return ctx.enter_context(nc.psum_tensor(name, shape, F32))

        def sem(name):
            return ctx.enter_context(nc.semaphore(name))

        pack = sb("pack", [P, PACK_COLS])
        gam = sb("gam", [P, TILES, T])
        expert_w = sb("expert_w", [P, LAYERS, EXPERTS + 1, HID])
        group_w = sb("group_w", [P, GROUPS_IMG, LAYERS, HID])
        sel = sb("sel", [P, STATES, P], BF16)
        wvo = sb("wvo", [P, D])
        wqk = sb("wqk", [P, P])
        w_mc = sb("w_mc", [P, 2, INNER])
        b_mc = sb("b_mc", [P, 1])
        neg_a = sb("neg_a", [P, STATES])
        route_i = sb("route_i", [EXPERTS, GROUPS], I32)
        route_f = sb("route_f", [EXPERTS, GROUPS])
        onehot = sb("onehot", [EXPERTS, GROUPS])
        route_ok = sb("route_ok", [1, 2, GROUPS])
        route_x = sb("route_x", [1, GROUPS], I32)
        group_b = sb("group_b", [P, LAYERS, GROUPS])
        ln_s = sb("ln_s", [P, 5, TILES])

        x_in = sb("x_in", [P, T])
        qT = sb("qT", [P, T])
        sp_pos = sb("sp_pos", [P, T])
        v_sb = sb("v_sb", [P, TILES, D])
        mixed = sb("mixed", [P, 2, T])
        pre = sb("pre", [P, 2, HALF])
        hT = sb("hT", [P, 2, HALF])
        bc = mixed[:, 0, :]
        xc = mixed[:, 1, :]
        gate = sb("gate", [P, 2, T])
        bc3 = sb("bc3", [P, 2, T], BF16)
        delta = sb("delta", [P, 2, T])
        u = sb("u", [P, 2, T])
        decay = sb("decay", [P, 2, T])
        ub = sb("ub", [P, 2, T])
        h = sb("h", [P, 3, T])
        c_row = sb("c_row", [P, 4, T])
        hc = sb("hc", [P, 2, T])
        y_t = sb("y_t", [P, T])
        h1T = y_t[:, 0:HALF]
        ln_x = sb("ln_x", [P, HALF])
        ln_q = sb("ln_q", [P, HALF])
        h1 = sb("h1", [P, HALF])
        h1b = sb("h1b", [P, HALF])
        f = sb("f", [P, T])
        yg = f
        res = ln_q

        acc_y = ps("acc_y", [P, T])
        b_row = ps("b_row", [P, T])
        work = ps("work", [P, T])
        acc_r = ps("acc_r", [P, HALF])
        tail = ps("tail", [P, HALF])

        c_dram = nc.dram_tensor("c_dram", (IMAGES, STATES, T), F32, kind="Internal").ap()

        def const(name, rows=P, row0=0):
            at, cols = PACK_AT[name]
            return pack[row0:row0 + rows, at:at + cols]

        ident = const("ident")
        w_bc4 = const("w_bc")

        s_pack = sem("first_constants_loaded")
        s_pack2 = sem("constants_loaded")
        s_gam = [sem(f"gamma_loaded_{j}") for j in range(TILES)]
        s_x = sem("x_loaded")
        s_route = sem("route_loaded")
        s_rw = sem("expert_weights_loaded")
        s_ones = sem("ones_row_set")
        s_sel0 = sem("selector_zeroed")
        s_sel = sem("selector_ready")
        s_wvo = sem("folded_weights_ready")
        s_mc0 = sem("conv_weights_zeroed")
        s_ea = sem("exp_a_ready")
        s_na = sem("neg_a_ready")
        s_rt = sem("route_steps")
        s_ri = sem("route_or_none_ready")
        s_ws = sem("shared_weights_ready")
        s_cw = sem("combined_weights_ready")
        s_gw = [sem(f"group_weights_loaded_{g}") for g in range(2)]

        work_full = sem("work_full")
        work_read = sem("work_read")
        tail_full = sem("tail_full")
        tail_read = sem("tail_read")
        side_full = sem("side_full")
        side_read = sem("side_read")
        v_full = sem("v_full")
        v_ready = sem("v_ready")
        gv_done = sem("mixed_used")
        prelu_part = sem("prelu_parts")
        h_ready = sem("h_ready")
        bc_hi = sem("bc_high_ready")
        bc_rest = sem("bc_rest_ready")
        bc_mid = sem("bc_middle_ready")
        bc_rest2 = sem("bc_rest2_ready")
        bc_split = sem("bc_split_ready")
        c_stored = sem("c_stored")
        sp_step = sem("softplus_steps")
        sp_pos_ready = sem("softplus_positive_ready")
        delta_ready = sem("delta_ready")
        u_ready = sem("u_ready")

        b_ready = sem("b_row_ready")
        decay_ready = sem("decay_ready")
        ub_ready = sem("ub_ready")
        scan_done = sem("scan_done")
        c_loaded = [sem(f"c_row_loaded_{i}") for i in range(4)]
        hc_ready = sem("hc_ready")
        hc_used = sem("hc_used")
        y_read = sem("y_read")

        ln_sum = sem("ln_sum")
        ln_cent = sem("ln_centred")
        ln_sq = sem("ln_squared")
        ln_var = sem("ln_variance")
        ln_std = sem("ln_variance_eps")
        ln_log = sem("ln_log_steps")
        ln_pow = sem("ln_scale_ready")
        ln_out = sem("ln_out")
        h1b_ready = sem("h1_with_bias")
        stored = sem("out_stored")

        PHASES = range(-1, IMAGES + 2)

        def last_steps(p, n):
            return [(b, m) for b, m in ((p - 2, n + STEPS), (p - 1, n)) if 0 <= b < IMAGES and m < LAST_STEPS]

        def step_of(p, n):
            head = p + 1 if p + 1 < IMAGES else None
            scan = p if 0 <= p < IMAGES else None
            return head, scan, last_steps(p, n), STEPS * p + n

        def work_use(image, use):
            return WORK_USES * image + use

        def tail_use(image, use):
            return TAIL_SETUP + TAIL_USES * image + use

        def tail_at(image, use):
            if image < ALONE:
                return tail[:, :], tail_full, tail_read, tail_use(image, use)
            before = TAIL_USES // 2 * (image - ALONE) + use // 2
            if use % 2 == 0:
                return tail[:, :], tail_full, tail_read, tail_use(ALONE, 0) + before
            return work[:, 0:HALF], side_full, side_read, before

        def tail_filled(image, use):
            _, full, _, before = tail_at(image, use)
            return full, before + 1

        def tail_taken(image, use):
            _, _, read, before = tail_at(image, use)
            return read, before + 1

        def tail_to_fill(image, n, half_step):
            return (TAIL_AT if image < ALONE else TAIL_AT_ALONE).get((n, half_step))

        def ln_at(image):
            return LN_AT if image < ALONE else LN_AT_ALONE

        def tail_to_read(image, n, half_step):
            return tail_to_fill(image, n, EARLY) if half_step == LATE else tail_to_fill(image, n - 1, LATE)

        def bcast(ap, shape):
            return ap.unsqueeze(2).broadcast_to(shape)

        block = ctx.enter_context(nc.Block())

        @block.sync
        def _(sp):
            sp.dma_start(x_in[0:D, :], xT[0]).then_inc(s_x, 16)
            sp.dma_start(gam[:, 0, :], gammaT[0:P, :]).then_inc(s_gam[0], 16)
            for j in range(1, TILES):
                sp.dma_start(gam[:, j, :], gammaT[j * P:(j + 1) * P, :]).then_inc(s_gam[j], 16)
            sp.dma_start(expert_w[:, :, 0:EXPERTS, :], routed_w).then_inc(s_rw, 16)

            def load_c(k):
                b, n = k // STEPS, k % STEPS
                if n == 0:
                    sp.wait_ge(c_stored, 16 * (b + 1))
                if k >= 4:
                    sp.wait_ge(hc_ready, k - 3)
                sp.dma_start(c_row[:, k % 4, :], c_dram[b, n, :].partition_broadcast(P)).then_inc(c_loaded[k % 4], 16)

            def load_group(b, g):
                if b >= 1:
                    sp.wait_ge(*tail_filled(b - 1, USE_L2 + g // 8))
                e = sp.value_load(route_x[0:1, GROUPS_IMG * b + g:GROUPS_IMG * b + g + 1],
                                  min_val=0, max_val=EXPERTS)
                sp.dma_start(group_w[:, g, :, :].unsqueeze(2), expert_w[:, :, bass.ds(e, 1), :])\
                    .then_inc(s_gw[g // 8], 16)

            for p in PHASES:
                for n in range(STEPS):
                    head, scan, last, k = step_of(p, n)
                    if head is not None and n == 11 and head + 1 < IMAGES:
                        sp.wait_ge(work_full, work_use(head, USE_CONV))
                        sp.dma_start(x_in[0:D, :], xT[head + 1]).then_inc(s_x, 16)
                    if head is not None and n == 14:
                        sp.wait_ge(work_read, work_use(head, USE_BC) + 2)
                        sp.dma_start(c_dram[head], mixed[STATES:2 * STATES, 0, :]).then_inc(c_stored, 16)
                    for ahead in {13: (), 14: (k + 2, k + 3)}.get(n, (k + 3,)):
                        if 0 <= ahead < STEPS * IMAGES:
                            load_c(ahead)
                    for b, m in last:
                        if m < 8:
                            if b == 0 and m == 0:
                                sp.wait_ge(s_rt, 5)
                                sp.wait_ge(s_cw, 3)
                            load_group(b, 2 * m)
                            load_group(b, 2 * m + 1)
                        if m == ln_at(b)[1] + 3:
                            sp.wait_ge(ln_out, 2 * b + 2)
                            for i in range(2):
                                sp.dma_start(out[b, i * HALF:(i + 1) * HALF, :].rearrange("(c t) d -> t c d", t=P),
                                             res[:, :].rearrange("p (c i d) -> p i c d", d=D, i=2)[:, i, :, :])\
                                    .then_inc(stored, 16)
            sp.wait_ge(stored, 32 * IMAGES)

        @block.tensor
        def _(pe):
            def warm_up(bank, operand, times):
                for _ in range(times):
                    nc.tensor.matmul(bank[:, 0:2 * INNER], operand[:, 0:P], operand, start=True, stop=True)

            pe.wait_ge(s_mc0, 1)
            warm_up(b_row, w_mc[:, :, :].rearrange("p i c -> p (i c)"), 5)
            pe.wait_ge(s_pack, 16)
            nc.tensor.matmul(tail[:, 0:D], const("wvb", D), const("wo_tok", D), start=True, stop=True)
            nc.tensor.matmul(tail[:, D:D + P], const("wqb", D), const("wkb", D), start=True, stop=True)
            nc.tensor.matmul(tail[:, 192:192 + INNER], const("w_main_t"), const("w_conv"), start=True, stop=True)
            nc.tensor.matmul(tail[:, 320:321], const("w_conv"), const("b_main"), start=True, stop=True)\
                .then_inc(tail_full, 1)

            def begin_work(image, use):
                if work_use(image, use) >= 2:
                    pe.wait_ge(work_read, work_use(image, use) - 1)

            def begin_tail(image, use):
                _, _, read, before = tail_at(image, use)
                if before:
                    pe.wait_ge(read, before)
                else:
                    pe.wait_ge(work_read, WORK_USES * IMAGES)
                if image >= ALONE:
                    for source in TAIL_FROM.get(use, ()):
                        pe.wait_ge(*tail_taken(image, source))

            def project(image, use, weights, moving):
                for i in range(2):
                    begin_work(image, use + i)
                    nc.tensor.matmul(work[:, i * HALF:(i + 1) * HALF], weights, moving[:, i * HALF:(i + 1) * HALF],
                                     start=True, stop=True).then_inc(work_full, 1)

            def states_in(k):
                b, n = k // STEPS, k % STEPS
                if n == 0:
                    pe.wait_ge(bc_split, b + 1)
                    if b == 0:
                        pe.wait_ge(s_sel, 1)
                if k:
                    pe.wait_ge(ub_ready, k)
                for i in range(2):
                    mm = nc.tensor.matmul(b_row[:, i * HALF:(i + 1) * HALF], sel[:, n, :],
                                          bc3[:, b % 2, i * HALF:(i + 1) * HALF], start=True, stop=True)
                mm.then_inc(b_ready, 1)

            def states_out(k):
                b, n = k // STEPS, k % STEPS
                pe.wait_ge(hc_ready, k + 1)
                if n == 0 and b:
                    pe.wait_ge(y_read, b)
                for c in range(TILES):
                    mm = nc.tensor.matmul(acc_y[:, c * P:(c + 1) * P], hc[:, k % 2, c * P:(c + 1) * P], ident,
                                          start=(n == 0 and c % 4 == 0), stop=(n == STATES - 1), is_transpose=True,
                                          skip_group_check=True)
                mm.then_inc(hc_used, 1)

            def queries(b):
                pe.wait_ge(s_x, 16 * (b + 1))
                if b == 0:
                    pe.wait_ge(s_ones, 2)
                    pe.wait_ge(s_wvo, 1)
                project(b, USE_Q, wqk[:, :], x_in)

            def values(b):
                if b == 0:
                    pe.wait_ge(s_wvo, 2)
                else:
                    pe.wait_ge(prelu_part, 2 * b)
                for c in range(TILES):
                    mm = nc.tensor.matmul(acc_r[:, c * D:(c + 1) * D], x_in[:, c * P:(c + 1) * P],
                                          wvo[:, :], start=True, stop=True)
                mm.then_inc(v_full, 1)

            def head_part(b, n):
                for unit in SCORES[n - 1] if n else ():
                    j = unit // 2
                    if unit % 2 == 0:
                        continue
                    pe.wait_ge(work_read, work_use(b, USE_S + unit) + 1)
                    if j == 0:
                        pe.wait_ge(v_ready, b + 1)
                    for i in range(2):
                        mm = nc.tensor.matmul(acc_r[D * i:D * i + D, :], v_sb[:, j, :],
                                              mixed[:, j % 2, i * HALF:(i + 1) * HALF],
                                              start=(j == 0), stop=(j == TILES - 1), skip_group_check=True)
                    mm.then_inc(gv_done, 1)

            def scores(b, n):
                for unit in SCORES[n + 1] if n + 1 < STEPS else ():
                    j, i = unit // 2, unit % 2
                    begin_work(b, USE_S + unit)
                    if unit == 0:
                        pe.wait_ge(work_read, work_use(b, USE_S))
                    nc.tensor.matmul(work[:, i * HALF:(i + 1) * HALF], x_in[:, j * P:(j + 1) * P],
                                     qT[:, i * HALF:(i + 1) * HALF], start=True, stop=True).then_inc(work_full, 1)

            def from_h(b, use, weights):
                for i in range(2):
                    begin_work(b, use + i)
                    nc.tensor.matmul(work[:, i * HALF:(i + 1) * HALF], weights(i), hT[:, b % 2, :],
                                     start=True, stop=True).then_inc(work_full, 1)

            def gate_product(b):
                if b == 0:
                    pe.wait_ge(s_pack2, 16)
                from_h(b, USE_GATE, lambda i: const("w_gate")[:, i * INNER:(i + 1) * INNER])

            def conv_product(b):
                warm_up(work, gam[:, 0, 0:2 * INNER], 3)
                pe.wait_ge(h_ready, b + 1)
                if b == 0:
                    pe.wait_ge(s_wvo, 4)
                from_h(b, USE_CONV, lambda i: w_mc[:, i, :])

            def head_late(b, n):
                if n == 9:
                    conv_product(b)
                if n == 10:
                    gate_product(b)
                if n == 11:
                    pe.wait_ge(work_read, work_use(b, USE_CONV) + 2)
                    project(b, USE_BC, const("w_bc"), xc)

            def head_early(b, n):
                if n == 12:
                    project(b, USE_DT, const("w_dt"), xc)

            def last_part(b, n, half_step):
                use = tail_to_fill(b, n, half_step)
                if use is None:
                    return
                if b == IMAGES - 1 and use == USE_H1:
                    warm_up(b_row, gam[:, 0, 0:2 * INNER], 7)
                if b == IMAGES - 1 and use == USE_OUT2:
                    warm_up(b_row, gam[:, 0, 0:2 * INNER], 2)
                begin_tail(b, use)
                bank = tail_at(b, use)[0]
                if use in (USE_YT, USE_YT + 1):
                    i = use - USE_YT
                    pe.wait_ge(y_read, b + 1)
                    for c in range(4 * i, 4 * i + 4):
                        mm = nc.tensor.transpose(bank[:, (c % 4) * P:(c % 4 + 1) * P], y_t[:, c * P:(c + 1) * P], ident)
                elif use == USE_OUT1:
                    for i in range(2):
                        mm = nc.tensor.matmul(bank[D * i:D * i + D, :], const("w_out"), yg[:, i * HALF:(i + 1) * HALF],
                                              start=True, stop=True, skip_group_check=True)
                elif use == USE_X1:
                    for c in range(TILES // 2):
                        mm = nc.tensor.transpose(bank[:, c * P:(c + 1) * P], yg[:, c * P:(c + 1) * P], ident)
                elif use == USE_H1:
                    pe.wait_ge(ln_out, 2 * b + 1)
                    for c in range(TILES // 2):
                        mm = nc.tensor.transpose(bank[:, c * P:(c + 1) * P], h1[:, c * P:(c + 1) * P], ident)
                elif use in (USE_F0, USE_F0 + 1):
                    i = use - USE_F0
                    mm = nc.tensor.matmul(bank[:, :], const("w_i", D, D * i), h1T[D * i:D * i + D, :],
                                          start=True, stop=True)
                elif use in (USE_L1, USE_L1 + 1, USE_L2, USE_L2 + 1):
                    layer, i = (use - USE_L1) // 2, (use - USE_L1) % 2
                    if layer == 0:
                        pe.wait_ge(s_gw[i], 16 * 8 * (b + 1))
                    for g in range(8 * i, 8 * i + 8):
                        mm = nc.tensor.matmul(bank[:, (g % 8) * GROUP:(g % 8 + 1) * GROUP], group_w[:, g, layer, :],
                                              f[:, g * GROUP:(g + 1) * GROUP], start=True, stop=True)
                elif use == USE_OUT2:
                    for c in range(TILES):
                        if b >= ALONE and c == (TILES // 2 if b == IMAGES - 1 else 0):
                            pe.wait_ge(*tail_taken(b, USE_L2 + 1))
                        at = (2 * (c % 4) + c // 4) * D
                        mm = nc.tensor.matmul(bank[:, at:at + D], f[:, c * P:(c + 1) * P], const("w_o"),
                                              start=True, stop=True)
                mm.then_inc(tail_filled(b, use)[0], 1)

            queries(0)
            values(0)
            for p in PHASES:
                for n in range(STEPS):
                    head, scan, last, k = step_of(p, n)
                    if 0 <= k + 1 < STEPS * IMAGES:
                        states_in(k + 1)
                    for b, m in last:
                        last_part(b, m, EARLY)
                    if head is not None:
                        head_early(head, n)
                    if 0 <= k - 2 < STEPS * IMAGES:
                        states_out(k - 2)
                    if head is not None:
                        head_part(head, n)
                    for b, m in last:
                        last_part(b, m, LATE)
                    if head is not None:
                        scores(head, n)
                        head_late(head, n)
                    if n == STEPS - 2 and p + 2 < IMAGES:
                        queries(p + 2)
                    if n == (STEPS - 2 if p == -1 else STEPS - 1) and p + 2 < IMAGES:
                        values(p + 2)
                    if p == -1 and n == 13:
                        pe.wait_ge(s_rt, 2)
                        pe.wait_ge(tail_read, 1)
                        for layer in range(LAYERS):
                            mm = nc.tensor.matmul(tail[:, layer * GROUPS:(layer + 1) * GROUPS],
                                                  const("b_r", EXPERTS)[:, layer * HID:(layer + 1) * HID],
                                                  onehot[:, :], start=True, stop=True)
                        mm.then_inc(tail_full, 1)

        @block.scalar
        def _(act):
            act.dma_start(pack[:, 0:PACK_FIRST], packed[:, 0:PACK_FIRST]).then_inc(s_pack, 16)
            act.dma_start(pack[:, PACK_FIRST:], packed[:, PACK_FIRST:]).then_inc(s_pack2, 16)
            act.preload_act_table_set("natural_log_exp_and_others")
            act.dma_start(route_i[:, :], route.partition_broadcast(EXPERTS)).then_inc(s_route, 16)
            act.wait_ge(s_pack, 16)
            nc.scalar.activation(neg_a[:, :], const("a_log"), ACT.Exp).then_inc(s_ea, 1)

            def decay_of(k):
                b, n = k // STEPS, k % STEPS
                if n == 0:
                    act.wait_ge(delta_ready, b + 1)
                    if b == 0:
                        act.wait_ge(s_na, 1)
                if k >= 2:
                    act.wait_ge(scan_done, k - 1)
                nc.scalar.activation(decay[:, k % 2, :], delta[:, b % 2, :], ACT.Exp, scale=neg_a[:, n:n + 1])\
                    .then_inc(decay_ready, 1)

            def halves(b, use, dst, func, **kw):
                for i in range(2):
                    act.wait_ge(work_full, work_use(b, use + i) + 1)
                    nc.scalar.activation(dst[:, i * HALF:(i + 1) * HALF], work[:, i * HALF:(i + 1) * HALF], func, **kw)\
                        .then_inc(work_read, 1)

            def gates(b):
                if b >= 2:
                    act.wait_ge(*tail_taken(b - 2, USE_YT + 1))
                halves(b, USE_GATE, gate[:, b % 2, :], ACT.Silu, bias=const("b_gate"))
                act.preload_act_table_set("natural_log_exp_and_others")

            def queries(b):
                if b:
                    act.wait_ge(bc_split, b)
                halves(b, USE_Q, qT, ACT.Copy)

            def head_part(b, n):
                if n == 0:
                    act.wait_ge(v_full, b + 1)
                    nc.scalar.activation(v_sb[:, :, :], acc_r[:, :].rearrange("p (c d) -> p c d", d=D), ACT.Copy)\
                        .then_inc(v_ready, 1)
                if n == 10:
                    act.preload_act_table_set("silu_and_others")
                    if b == 0:
                        act.wait_ge(s_wvo, 5)
                        act.wait_ge(s_pack2, 16)
                    halves(b, USE_CONV, xc, ACT.Silu, bias=b_mc[:, :])
                if n == 12:
                    act.wait_ge(work_read, work_use(b, USE_BC) + 2)
                    if b >= 2:
                        act.wait_ge(b_ready, STEPS * (b - 1))
                    nc.scalar.activation(bc3[:, b % 2, :], bc, ACT.Copy).then_inc(bc_hi, 1)
                if n == 13:
                    if b >= 2:
                        act.wait_ge(decay_ready, STEPS * (b - 1))
                    for i in range(2):
                        act.wait_ge(sp_pos_ready, 2 * b + i + 1)
                        at = slice(i * HALF, (i + 1) * HALF)
                        nc.scalar.activation(delta[:, b % 2, at], work[:, at], ACT.Abs, bias=const("b_dt"))\
                            .then_inc(work_read, 1)
                    act.wait_ge(work_read, work_use(b, USE_DT) + 2)
                    nc.scalar.activation(delta[:, b % 2, :], delta[:, b % 2, :], ACT.Exp, scale=-1.0)\
                        .then_inc(sp_step, 1)
                    act.wait_ge(bc_rest, b + 1)
                    nc.scalar.activation(bc3[D:P, b % 2, :], qT[D:P, :], ACT.Copy).then_inc(bc_mid, 1)

            def last_part(b, n, half_step):
                if (n, half_step) == (1, LATE):
                    act.wait_ge(hc_used, STEPS * (b + 1))
                    nc.scalar.activation(y_t[:, :], acc_y[:, :], ACT.Copy).then_inc(y_read, 1)
                if half_step == LATE and n in ln_at(b):
                    if n == ln_at(b)[0]:
                        act.wait_ge(*tail_taken(b, USE_X1))
                    else:
                        act.wait_ge(ln_cent, b + 1)
                    if b:
                        act.wait_ge(stored, 32 * b)
                    nc.scalar.activation(ln_q[:, :], ln_x[:, :], ACT.Square).then_inc(ln_sq, 1)
                if half_step == EARLY and n - 2 in ln_at(b):
                    count = 2 * b + ln_at(b).index(n - 2)
                    act.wait_ge(ln_std, count + 1)
                    nc.scalar.activation(ln_s[:, 3, :], ln_s[:, 2, :], ACT.Ln).then_inc(ln_log, 1)
                    act.wait_ge(ln_log, 2 * count + 1)
                    nc.scalar.activation(ln_s[:, 3, :], ln_s[:, 3, :], ACT.Exp, scale=-0.5).then_inc(ln_log, 1)
                use = tail_to_read(b, n, half_step)
                bank = None if use is None else tail_at(b, use)[0]
                if use == USE_H1:
                    act.wait_ge(*tail_filled(b, use))
                    nc.scalar.activation(h1T, bank[:, :], ACT.Copy).then_inc(tail_taken(b, use)[0], 1)
                if use in (USE_F0, USE_F0 + 1):
                    i = use - USE_F0
                    act.wait_ge(*tail_filled(b, use))
                    nc.scalar.activation(f[:, i * HALF:(i + 1) * HALF], bank[:, :], ACT.Relu, bias=const("b_i"))\
                        .then_inc(tail_taken(b, use)[0], 1)
                if use in (USE_L2, USE_L2 + 1):
                    layer, i = 1, use - USE_L2
                    act.wait_ge(*tail_filled(b, use))
                    for g in range(8 * i, 8 * i + 8):
                        op = nc.scalar.activation(f[:, g * GROUP:(g + 1) * GROUP],
                                                  bank[:, (g % 8) * GROUP:(g % 8 + 1) * GROUP], ACT.Relu,
                                                  bias=group_b[:, layer, GROUPS_IMG * b + g:GROUPS_IMG * b + g + 1])
                    op.then_inc(tail_taken(b, use)[0], 1)

            queries(0)
            for p in PHASES:
                for n in range(STEPS):
                    head, scan, last, k = step_of(p, n)
                    if head is not None and n == 11:
                        gates(head)
                    if 0 <= k + 1 < STEPS * IMAGES:
                        decay_of(k + 1)
                    if head is not None and n == 14:
                        b = head
                        act.wait_ge(sp_step, 2 * b + 1)
                        nc.scalar.activation(delta[:, b % 2, :], delta[:, b % 2, :], ACT.Ln, bias=1.0)\
                            .then_inc(sp_step, 1)
                        act.wait_ge(bc_rest2, head + 1)
                        nc.scalar.activation(bc3[96:P, head % 2, :], qT[96:P, :], ACT.Copy).then_inc(bc_split, 1)
                    for b, m in last:
                        last_part(b, m, EARLY)
                    if head is not None:
                        head_part(head, n)
                    for b, m in last:
                        last_part(b, m, LATE)
                    if n == STEPS - 1 and p + 2 < IMAGES:
                        queries(p + 2)

        @block.gpsimd
        def _(pool):
            nc.gpsimd.memset(sel[:, :, :], 0.0).then_inc(s_sel0, 1)
            for i, lo in enumerate((0, 64, 96)):
                pool.wait_ge(s_sel0, i + 1)
                nc.gpsimd.affine_select(out=sel[:, :, :], in_=sel[:, :, :], compare_op=ALU.not_equal, fill=1.0,
                                        base=-lo, pattern=[[-1, STATES], [0, P]], channel_multiplier=1)\
                    .then_inc(s_sel if lo == 96 else s_sel0, 1)

            def combine_weights():
                pool.wait_ge(s_pack2, 16)
                for layer in range(LAYERS):
                    at = PACK_AT["w_s"][0] + layer * HID
                    nc.gpsimd.tensor_tensor(expert_w[:, layer, EXPERTS, :], pack[:, at:at + HID], ident, ALU.add)\
                        .then_inc(s_ws, 1)
                pool.wait_ge(s_ws, 2)
                pool.wait_ge(s_rw, 16)
                for layer in range(LAYERS):
                    w = expert_w[:, layer, 0:EXPERTS, :]
                    nc.gpsimd.tensor_tensor(w, w, expert_w[:, layer, EXPERTS, :].unsqueeze(1)
                                            .broadcast_to([P, EXPERTS, HID]), ALU.add).then_inc(s_cw, 1)
                pool.wait_ge(s_cw, 2)
                pool.sem_inc(s_cw, 1)

            def weigh(k):
                pool.wait_ge(scan_done, k + 1)
                pool.wait_ge(c_loaded[k % 4], 16 * (k // 4 + 1))
                if k >= 2:
                    pool.wait_ge(hc_used, k - 1)
                nc.gpsimd.tensor_tensor(hc[:, k % 2, :], h[:, k % 3, :], c_row[:, k % 4, :], ALU.mult)\
                    .then_inc(hc_ready, 1)

            def head_part(b, n):
                if n == 12 and b:
                    pool.wait_ge(bc_hi, b + 1)
                    nc.gpsimd.tensor_tensor(qT[:, :], bc, bc3[:, b % 2, :], ALU.subtract).then_inc(bc_rest, 1)
                if n == 13 and b:
                    pool.wait_ge(bc_mid, b + 1)
                    nc.gpsimd.tensor_tensor(qT[:, :], qT[:, :], bc3[:, b % 2, :], ALU.subtract).then_inc(bc_rest2, 1)

            def last_part(b, n):
                if n == 10:
                    pool.wait_ge(ln_out, 2 * b + 1)
                    if b:
                        pool.wait_ge(*tail_taken(b - 1, USE_OUT2))
                    nc.gpsimd.tensor_tensor(h1b[:, :].rearrange("p (c d) -> p c d", d=D),
                                            h1[:, :].rearrange("p (c d) -> p c d", d=D),
                                            const("b_o").unsqueeze(1).broadcast_to([P, TILES, D]), ALU.add)\
                        .then_inc(h1b_ready, 1)

            for p in PHASES:
                for n in range(STEPS):
                    head, scan, last, k = step_of(p, n)
                    if 0 <= k - 1 < STEPS * IMAGES:
                        weigh(k - 1)
                    if head is not None:
                        head_part(head, n)
                    for b, m in last:
                        last_part(b, m)
                    if p == -1 and n == 10:
                        combine_weights()

        @block.vector
        def _(dve):
            nc.vector.memset(w_mc[:, :, :], 0.0).then_inc(s_mc0, 1)
            nc.vector.memset(x_in[D:P, :], 0.0).then_inc(s_ones, 1)
            dve.wait_ge(s_ones, 1)
            nc.vector.memset(x_in[D:D + 1, :], 1.0).then_inc(s_ones, 1)
            dve.wait_ge(tail_full, 1)
            dve.wait_ge(s_pack, 16)
            nc.vector.tensor_copy(wqk[:, :], tail[:, D:D + P]).then_inc(s_wvo, 1)
            nc.vector.tensor_copy(wvo[:, :], tail[:, 0:D]).then_inc(s_wvo, 1)
            dve.wait_ge(s_mc0, 1)
            for i in range(2):
                nc.vector.tensor_copy(w_mc[D * i:D * i + D, i, :], tail[D * i:D * i + D, 192:192 + INNER])\
                    .then_inc(s_wvo, 1)
            nc.vector.tensor_tensor(b_mc[:, :], tail[:, 320:321], const("b_conv"), ALU.add).then_inc(s_wvo, 1)
            dve.wait_ge(s_wvo, 5)
            dve.sem_inc(tail_read, 1)
            dve.wait_ge(s_ea, 1)
            nc.vector.tensor_scalar(neg_a[:, :], neg_a[:, :], -1.0, None, ALU.mult).then_inc(s_na, 1)

            def routes():
                dve.wait_ge(s_route, 16)
                dve.wait_ge(s_pack2, 16)
                nc.vector.tensor_copy(route_f[:, :], route_i[:, :]).then_inc(s_rt, 1)
                dve.wait_ge(s_rt, 1)
                nc.vector.tensor_scalar(onehot[:, :], route_f[:, :], const("expert", EXPERTS), None, ALU.is_equal)\
                    .then_inc(s_rt, 1)
                nc.vector.tensor_scalar(route_ok[:, 0, :], route_f[0:1, :], 0.0, None, ALU.is_ge).then_inc(s_rt, 1)
                dve.wait_ge(s_rt, 3)
                nc.vector.scalar_tensor_tensor(out=route_ok[:, 1, :], in0=route_f[0:1, :], scalar=float(EXPERTS - 1),
                                               in1=route_ok[:, 0, :], op0=ALU.is_le, op1=ALU.mult).then_inc(s_rt, 1)
                dve.wait_ge(s_rt, 4)
                nc.vector.scalar_tensor_tensor(out=route_ok[:, 0, :], in0=route_f[0:1, :], scalar=float(EXPERTS),
                                               in1=route_ok[:, 1, :], op0=ALU.subtract, op1=ALU.mult)\
                    .then_inc(s_ri, 1)
                dve.wait_ge(s_ri, 1)
                nc.vector.tensor_scalar(route_x[:, :], route_ok[:, 0, :], float(EXPERTS), None, ALU.add)\
                    .then_inc(s_rt, 1)

            def group_bias():
                dve.wait_ge(tail_full, 2)
                for layer in range(LAYERS):
                    at = PACK_AT["b_s"][0] + layer
                    op = nc.vector.tensor_scalar(group_b[:, layer, :], tail[:, layer * GROUPS:(layer + 1) * GROUPS],
                                                 pack[:, at:at + 1], None, ALU.add)
                op.then_inc(tail_read, 1)

            def drive(k):
                b, n = k // STEPS, k % STEPS
                if n == 0:
                    dve.wait_ge(u_ready, b + 1)
                dve.wait_ge(b_ready, k + 1)
                if k >= 2:
                    dve.wait_ge(scan_done, k - 1)
                nc.vector.tensor_tensor(ub[:, k % 2, :], u[:, b % 2, :], b_row[:, :], ALU.mult).then_inc(ub_ready, 1)

            def scan_step(k):
                dve.wait_ge(ub_ready, k + 1)
                dve.wait_ge(decay_ready, k + 1)
                if k >= 3:
                    dve.wait_ge(hc_ready, k - 2)
                nc.vector.tensor_tensor_scan(h[:, k % 3, :], decay[:, k % 2, :], ub[:, k % 2, :], 0.0,
                                             ALU.mult, ALU.add).then_inc(scan_done, 1)

            def head_part(b, n):
                for unit in SCORES[n]:
                    j, i = unit // 2, unit % 2
                    at = slice(i * HALF, (i + 1) * HALF)
                    if b == 0:
                        dve.wait_ge(s_gam[j], 16)
                    dve.wait_ge(work_full, work_use(b, USE_S + unit) + 1)
                    if b and unit == 0:
                        dve.wait_ge(bc_rest, b)
                        dve.wait_ge(c_stored, 16 * b)
                    if b and unit == 2:
                        dve.wait_ge(u_ready, b)
                    if TILES * b + j >= 2 and i == 0:
                        dve.wait_ge(gv_done, TILES * b + j - 1)
                    nc.vector.tensor_tensor(mixed[:, j % 2, at], gam[:, j, at], work[:, at], ALU.mult)\
                        .then_inc(work_read, 1)

            def prelu(b):
                dve.wait_ge(gv_done, TILES * (b + 1))
                for i, op in enumerate((ALU.min, ALU.max)):
                    nc.vector.tensor_scalar(pre[:, i, :], acc_r[:, :], const("bo_tok"), 0.0, ALU.add, op)\
                        .then_inc(prelu_part, 1)
                dve.wait_ge(prelu_part, 2 * b + 2)
                if b >= 2:
                    dve.wait_ge(*tail_taken(b - 2, USE_OUT1))
                nc.vector.scalar_tensor_tensor(out=hT[:, b % 2, :], in0=pre[:, 0, :], scalar=const("prelu_a"),
                                               in1=pre[:, 1, :], op0=ALU.mult, op1=ALU.add).then_inc(h_ready, 1)

            def states(b):
                for i in range(2):
                    dve.wait_ge(work_full, work_use(b, USE_BC + i) + 1)
                    dve.wait_ge(work_read, work_use(b, USE_BC + i))
                    at = slice(i * HALF, (i + 1) * HALF)
                    nc.vector.tensor_scalar(bc[:, at], work[:, at], const("b_bc"), None, ALU.add).then_inc(work_read, 1)

            def step_sizes(b):
                if b:
                    dve.wait_ge(delta_ready, b)
                for i in range(2):
                    dve.wait_ge(work_full, work_use(b, USE_DT + i) + 1)
                    at = slice(i * HALF, (i + 1) * HALF)
                    nc.vector.tensor_scalar(sp_pos[:, at], work[:, at], const("b_dt"), 0.0, ALU.add, ALU.max)\
                        .then_inc(sp_pos_ready, 1)

            def rows(ap):
                return ap.rearrange("p (c d) -> p c d", d=D)

            def norm(count, part, dst, src=None):
                x3 = rows(ln_x[:, :])
                if part == 0:
                    nc.vector.tensor_reduce(ln_s[:, 0, :], src, AX.X, ALU.add).then_inc(ln_sum, 1)
                    dve.wait_ge(ln_sum, count + 1)
                    nc.vector.scalar_tensor_tensor(out=x3, in0=bcast(ln_s[:, 0, :], [P, TILES, D]), scalar=-1.0 / D,
                                                   in1=src, op0=ALU.mult, op1=ALU.add)\
                        .then_inc(tail_taken(count // 2, USE_X1)[0] if count % 2 == 0 else ln_cent, 1)
                if part == 1:
                    dve.wait_ge(ln_sq, count + 1)
                    nc.vector.tensor_reduce(ln_s[:, 1, :], rows(ln_q[:, :]), AX.X, ALU.add).then_inc(ln_var, 1)
                    dve.wait_ge(ln_var, count + 1)
                    nc.vector.tensor_scalar(ln_s[:, 2, :], ln_s[:, 1, :], 1.0 / D, EPS, ALU.mult, ALU.add)\
                        .then_inc(ln_std, 1)
                if part == 2:
                    v, r, t = ln_s[:, 2, :], ln_s[:, 3, :], ln_s[:, 4, :]
                    dve.wait_ge(ln_log, 2 * count + 2)
                    nc.vector.tensor_tensor(t, r, r, ALU.mult).then_inc(ln_pow, 1)
                    dve.wait_ge(ln_pow, 3 * count + 1)
                    nc.vector.scalar_tensor_tensor(out=t, in0=t, scalar=-0.5, in1=v, op0=ALU.mult, op1=ALU.mult)\
                        .then_inc(ln_pow, 1)
                    dve.wait_ge(ln_pow, 3 * count + 2)
                    nc.vector.scalar_tensor_tensor(out=r, in0=t, scalar=1.5, in1=r, op0=ALU.add, op1=ALU.mult)\
                        .then_inc(ln_pow, 1)
                    dve.wait_ge(ln_pow, 3 * count + 3)
                    nc.vector.tensor_tensor(dst, x3, bcast(ln_s[:, 3, :], [P, TILES, D]), ALU.mult).then_inc(ln_out, 1)

            def last_part(b, n, half_step):
                use = tail_to_read(b, n, half_step)
                bank = None if use is None else tail_at(b, use)[0]
                if use in (USE_YT, USE_YT + 1):
                    at = slice((use - USE_YT) * HALF, (use - USE_YT + 1) * HALF)
                    dve.wait_ge(*tail_filled(b, use))
                    dve.wait_ge(work_read, work_use(b, USE_GATE) + 2)
                    nc.vector.tensor_tensor(yg[:, at], gate[:, b % 2, at], bank[:, :], ALU.mult)\
                        .then_inc(tail_taken(b, use)[0], 1)
                if use == USE_OUT1:
                    dve.wait_ge(*tail_filled(b, use))
                    nc.vector.scalar_tensor_tensor(out=yg[:, 0:HALF], in0=bank[:, :], scalar=const("b_out"),
                                                   in1=hT[:, b % 2, :], op0=ALU.add, op1=ALU.add)\
                        .then_inc(tail_taken(b, use)[0], 1)
                if use == USE_X1:
                    dve.wait_ge(*tail_filled(b, use))
                    norm(2 * b, 0, None, rows(bank[:, :]))
                if use in (USE_L1, USE_L1 + 1):
                    i = use - USE_L1
                    dve.wait_ge(*tail_filled(b, use))
                    for g in range(8 * i, 8 * i + 8):
                        at = GROUPS_IMG * b + g
                        op = nc.vector.tensor_scalar(f[:, g * GROUP:(g + 1) * GROUP],
                                                     bank[:, (g % 8) * GROUP:(g % 8 + 1) * GROUP],
                                                     group_b[:, 0, at:at + 1], 0.0, ALU.add, ALU.max)
                    op.then_inc(tail_taken(b, use)[0], 1)
                if use == USE_OUT2:
                    dve.wait_ge(*tail_filled(b, use))
                    dve.wait_ge(h1b_ready, b + 1)
                    nc.vector.tensor_tensor(ln_x[:, :], bank[:, :], h1b[:, :], ALU.add)\
                        .then_inc(tail_taken(b, use)[0], 1)
                    dve.wait_ge(*tail_taken(b, use))
                    norm(2 * b + 1, 0, None, rows(ln_x[:, :]))
                if (n, half_step) == (ln_at(b)[0] + 1, LATE):
                    norm(2 * b, 1, None)
                if (n, half_step) == (ln_at(b)[0] + 3, EARLY):
                    if b:
                        dve.wait_ge(h1b_ready, b)
                    norm(2 * b, 2, rows(h1[:, :]))
                if (n, half_step) == (ln_at(b)[1] + 1, LATE):
                    norm(2 * b + 1, 1, None)
                if (n, half_step) == (ln_at(b)[1] + 3, EARLY):
                    norm(2 * b + 1, 2, rows(res[:, :]))

            for p in PHASES:
                for n in range(STEPS):
                    head, scan, last, k = step_of(p, n)
                    if scan is not None:
                        drive(k)
                    if head is not None and n == 12:
                        states(head)
                    if head is not None and n == 13:
                        step_sizes(head)
                    if head == 0 and n == 13:
                        dve.wait_ge(bc_hi, 1)
                        nc.vector.tensor_tensor(qT[:, :], bc, bc3[:, 0, :], ALU.subtract).then_inc(bc_rest, 1)
                        dve.wait_ge(bc_mid, 1)
                        nc.vector.tensor_tensor(qT[:, :], qT[:, :], bc3[:, 0, :], ALU.subtract).then_inc(bc_rest2, 1)
                    if head is not None and n == 15:
                        dve.wait_ge(sp_step, 2 * head + 2)
                        nc.vector.tensor_tensor(delta[:, head % 2, :], delta[:, head % 2, :], sp_pos[:, :], ALU.add)\
                            .then_inc(delta_ready, 1)
                    if head is not None:
                        for b, m in last:
                            last_part(b, m, EARLY)
                        head_part(head, n)
                    if scan is not None:
                        scan_step(k)
                    if head is None:
                        for b, m in last:
                            last_part(b, m, EARLY)
                    for b, m in last:
                        last_part(b, m, LATE)
                    if head is not None and n == 9:
                        prelu(head)
                    if head is not None and n == 15:
                        dve.wait_ge(delta_ready, head + 1)
                        nc.vector.tensor_tensor(u[:, head % 2, :], delta[:, head % 2, :], xc, ALU.mult)\
                            .then_inc(u_ready, 1)
                    if p == -1 and n == 1:
                        routes()
                    if p == -1 and n == 13:
                        group_bias()


def kernel(**inputs):
    import numpy as np
    import concourse.bacc as bacc
    from concourse.bass_utils import run_bass_kernel_spmd

    a = {name: np.ascontiguousarray(value) for name, value in inputs.items()}
    tok = {n[len("L0_tok_"):]: v for n, v in a.items() if n.startswith("L0_tok_")}
    att = {n[len("L0_attn_"):]: v for n, v in a.items() if n.startswith("L0_attn_")}
    ffn = {n[len("L0_ffn_"):]: v for n, v in a.items() if n.startswith("L0_ffn_")}

    packed = np.zeros((P, PACK_COLS), np.float32)

    def place(name, value, row0=0, col0=0):
        at = PACK_AT[name][0] + col0
        packed[row0:row0 + value.shape[0], at:at + value.shape[1]] = value

    for name, w, b in (("wqb", tok["Wq"], tok["bq"]), ("wkb", tok["Wk"], tok["bk"]), ("wvb", tok["Wv"], tok["bv"])):
        place(name, w.T)
        place(name, b[:, None], 0, D)
    for i in range(2):
        place("w_main_t", att["W_in"][:, 0:INNER].T, 0, D * i)
        place("w_gate", att["W_in"][:, INNER:], D * i, INNER * i)
        place("bo_tok", tok["bo"][:, None], D * i)
    place("b_main", att["b_in"][0:INNER, None])
    place("b_gate", att["b_in"][INNER:, None])
    place("wo_tok", tok["Wo"])
    place("prelu_a", np.broadcast_to(tok["prelu_a"].reshape(1, 1), (P, 1)))
    place("ident", np.eye(P, dtype=np.float32))
    place("w_conv", att["W_conv"])
    place("b_conv", att["b_conv"][:, None])
    for i in range(4):
        place("w_bc", att["W_bc"], 0, 2 * STATES * i)
        place("b_bc", att["b_bc"][:, None], 2 * STATES * i)
    place("w_dt", att["W_dt"])
    place("b_dt", att["b_dt"][:, None])
    place("a_log", att["A_log"])
    place("w_out", att["W_out"])
    for i in range(2):
        place("b_out", att["b_out"][:, None], D * i)
        place("w_i", ffn["Wi"].T, D * i)
    place("b_i", ffn["bi"][:, None])
    place("w_o", ffn["Wo"].T)
    place("b_o", np.broadcast_to(ffn["bo"], (P, D)))
    for layer in range(LAYERS):
        place("b_r", ffn["br"][layer], 0, HID * layer)
        place("b_s", ffn["bs"][layer, 0][:, None], 0, layer)
        place("w_s", ffn["Ws"][layer, 0].T, 0, HID * layer)
    place("expert", np.arange(EXPERTS, dtype=np.float32)[:, None])

    arrays = {
        "xT": np.ascontiguousarray(a["x"].reshape(IMAGES, T, D).transpose(0, 2, 1)),
        "gammaT": np.ascontiguousarray(tok["d_gamma_batched"].T),
        "packed": packed,
        "routed_w": np.ascontiguousarray(ffn["Wr"].transpose(3, 0, 1, 2)),
        "route": ffn["route_id"],
    }
    nc = bacc.Bacc("TRN2", target_bir_lowering=False, num_devices=1)
    args = [nc.dram_tensor(name, v.shape, mybir.dt.from_np(v.dtype), kind="ExternalInput").ap()
            for name, v in arrays.items()]
    out = nc.dram_tensor("out", (IMAGES, T, D), F32, kind="ExternalOutput").ap()
    vit_layer(nc, *args, out)
    result = run_bass_kernel_spmd(nc, [arrays], core_ids=[0])
    return result.results[0]["out"]
```
